# Optimizing a Trainium2 kernel written in Bass

```python
import numpy as np
import jax
import jax.numpy as jnp

def _softmax(x, axis=-1):
    return jax.nn.softmax(x, axis=axis)

def _gelu(x):
    return jax.nn.gelu(x, approximate=True)

def _silu(x):
    return jax.nn.silu(x)

def _sigmoid(x):
    return jax.nn.sigmoid(x)

def _layernorm(x, axis=-1, eps=1e-05):
    m = jnp.mean(x, axis=axis, keepdims=True)
    v = jnp.var(x, axis=axis, keepdims=True)
    return (x - m) / jnp.sqrt(v + eps)

def _scatter_add(tgt, idx, src, axis=0):
    return tgt.at[idx].add(src)

def _segment_sum(src, seg, n):
    return jax.ops.segment_sum(src, seg, n)
kernel_name = 'mk_seq_postln_d1_jaxref_r4_55e439'

def setup_inputs(seed: int=0):
    np.random.seed(seed)
    _w = jnp.asarray

    def _L0_attn_setup():
        import jax, jax.numpy as jnp
        import numpy as np
        B, T, D = (1, 512, 256)
        H, S, LV = (16, 64, 12)
        HD = D // H
        NEG = -1e+30

        def _level_matrix(length, num_levels):
            t = np.arange(length)
            xor = t[:, None] ^ t[None, :]
            lv = np.zeros((length, length), dtype=np.int32)
            for k in range(num_levels - 1):
                lv += (xor >= 1 << k).astype(np.int32)
            return jnp.asarray(lv)

        def _forward(x, Wq, Wk, Wv, Wdl, Wdt, Wout, A_log, dt_bias, Lp, ln_g, ln_b):
            Bb, Tt, Dd = x.shape
            Q = (x @ Wq.T).reshape(Bb, Tt, H, S)
            K = (x @ Wk.T).reshape(Bb, Tt, H, S)
            V = (x @ Wv.T).reshape(Bb, Tt, H, HD)
            dl = (x @ Wdl.T).reshape(Bb, Tt, H, LV)
            A = -jnp.exp(A_log)
            dt = jax.nn.softplus(x @ Wdt.T + dt_bias)
            g = A[None, None, :] * dt
            Lam = jax.nn.softplus(Lp[None, None] * dl)
            cg = jnp.cumsum(g, axis=1)
            diff = cg[:, :, None, :] - cg[:, None, :, :]
            tri = np.tril(np.ones((Tt, Tt), dtype=bool))
            decay = jnp.exp(jnp.where(tri[None, :, :, None], diff, NEG))
            levels = _level_matrix(Tt, LV)
            lam_ts = jnp.take_along_axis(Lam[:, :, :, None, :], levels[None, :, None, :, None], axis=-1)[..., 0]
            scores = jnp.einsum('bthd,bshd->bhts', Q, K) * S ** (-0.5)
            Wmat = scores * jnp.transpose(decay, (0, 3, 1, 2)) * jnp.transpose(lam_ts, (0, 2, 1, 3))
            Y = jnp.einsum('bhts,bshd->bthd', Wmat, V).reshape(Bb, Tt, H * HD)
            o = Y @ Wout.T + x
            mu = o.mean(-1, keepdims=True)
            var = ((o - mu) ** 2).mean(-1, keepdims=True)
            return (o - mu) * jax.lax.rsqrt(var + 1e-05) * ln_g + ln_b
        ks = jax.random.split(jax.random.key(seed), 8)
        n = jax.random.normal
        w = 0.02
        return {'x': n(ks[0], (B, T, D), jnp.float32), 'Wq': n(ks[1], (H * S, D), jnp.float32) * w, 'Wk': n(ks[2], (H * S, D), jnp.float32) * w, 'Wv': n(ks[3], (H * HD, D), jnp.float32) * w, 'Wdl': n(ks[4], (H * LV, D), jnp.float32) * w, 'Wdt': n(ks[5], (H, D), jnp.float32) * w, 'Wout': n(ks[6], (D, H * HD), jnp.float32) * w, 'A_log': jnp.log(jnp.arange(1, H + 1, dtype=jnp.float32)), 'dt_bias': n(ks[7], (H,), jnp.float32), 'Lp': jnp.ones((H, LV), jnp.float32), 'ln_g': jnp.ones((D,), jnp.float32), 'ln_b': jnp.zeros((D,), jnp.float32)}
    _L0_attn_in = _L0_attn_setup()

    def _L0_ffn_setup():
        import jax, jax.numpy as jnp
        import numpy as np
        from jax import lax
        T, B, I, M, O = (64, 64, 256, 256, 256)

        def _xavier(key, shape):
            fan_out, fan_in = shape
            limit = float(np.sqrt(6.0 / (fan_in + fan_out)))
            return jax.random.uniform(key, shape, jnp.float32, -limit, limit)
        key = jax.random.key(seed)
        ks = jax.random.split(key, 9)
        x = jax.random.normal(ks[0], (T, B, I), jnp.float32)
        return {'x': x, 'wf': _xavier(ks[1], (M, I)), 'uf': _xavier(ks[2], (M, M)), 'bf': jnp.zeros((M,), jnp.float32), 'wi': _xavier(ks[3], (M, I)), 'ui': _xavier(ks[4], (M, M)), 'bi': jnp.zeros((M,), jnp.float32), 'wc': _xavier(ks[5], (M, I)), 'uc': _xavier(ks[6], (M, M)), 'bc': jnp.zeros((M,), jnp.float32), 'wo': _xavier(ks[7], (O, I)), 'uo': _xavier(ks[8], (O, M)), 'bo': jnp.zeros((O,), jnp.float32), 'in_c': jnp.zeros((M,), jnp.float32)}
    _L0_ffn_in = _L0_ffn_setup()
    _d = {'L0_attn_x': _L0_attn_in['x'], 'L0_attn_Wq': _L0_attn_in['Wq'], 'L0_attn_Wk': _L0_attn_in['Wk'], 'L0_attn_Wv': _L0_attn_in['Wv'], 'L0_attn_Wdl': _L0_attn_in['Wdl'], 'L0_attn_Wdt': _L0_attn_in['Wdt'], 'L0_attn_Wout': _L0_attn_in['Wout'], 'L0_attn_A_log': _L0_attn_in['A_log'], 'L0_attn_dt_bias': _L0_attn_in['dt_bias'], 'L0_attn_Lp': _L0_attn_in['Lp'], 'L0_attn_ln_g': _L0_attn_in['ln_g'], 'L0_attn_ln_b': _L0_attn_in['ln_b'], 'L0_ffn_wf': _L0_ffn_in['wf'], 'L0_ffn_uf': _L0_ffn_in['uf'], 'L0_ffn_bf': _L0_ffn_in['bf'], 'L0_ffn_wi': _L0_ffn_in['wi'], 'L0_ffn_ui': _L0_ffn_in['ui'], 'L0_ffn_bi': _L0_ffn_in['bi'], 'L0_ffn_wc': _L0_ffn_in['wc'], 'L0_ffn_uc': _L0_ffn_in['uc'], 'L0_ffn_bc': _L0_ffn_in['bc'], 'L0_ffn_wo': _L0_ffn_in['wo'], 'L0_ffn_uo': _L0_ffn_in['uo'], 'L0_ffn_bo': _L0_ffn_in['bo'], 'L0_ffn_in_c': _L0_ffn_in['in_c']}
    _x0 = _d['L0_attn_x']
    _d['L0_attn_x'] = jax.random.normal(jax.random.fold_in(jax.random.key(seed), 1), (2, 2048, 256), dtype=_x0.dtype)
    del _x0
    return _d

def reference(L0_attn_x, L0_attn_Wq, L0_attn_Wk, L0_attn_Wv, L0_attn_Wdl, L0_attn_Wdt, L0_attn_Wout, L0_attn_A_log, L0_attn_dt_bias, L0_attn_Lp, L0_attn_ln_g, L0_attn_ln_b, L0_ffn_wf, L0_ffn_uf, L0_ffn_bf, L0_ffn_wi, L0_ffn_ui, L0_ffn_bi, L0_ffn_wc, L0_ffn_uc, L0_ffn_bc, L0_ffn_wo, L0_ffn_uo, L0_ffn_bo, L0_ffn_in_c):

    def _L0_attn_ref(x, Wq, Wk, Wv, Wdl, Wdt, Wout, A_log, dt_bias, Lp, ln_g, ln_b):
        import jax, jax.numpy as jnp
        import numpy as np
        B, T, D = (1, 512, 256)
        H, S, LV = (16, 64, 12)
        HD = D // H
        NEG = -1e+30

        def _level_matrix(length, num_levels):
            t = np.arange(length)
            xor = t[:, None] ^ t[None, :]
            lv = np.zeros((length, length), dtype=np.int32)
            for k in range(num_levels - 1):
                lv += (xor >= 1 << k).astype(np.int32)
            return jnp.asarray(lv)

        def _forward(x, Wq, Wk, Wv, Wdl, Wdt, Wout, A_log, dt_bias, Lp, ln_g, ln_b):
            Bb, Tt, Dd = x.shape
            Q = (x @ Wq.T).reshape(Bb, Tt, H, S)
            K = (x @ Wk.T).reshape(Bb, Tt, H, S)
            V = (x @ Wv.T).reshape(Bb, Tt, H, HD)
            dl = (x @ Wdl.T).reshape(Bb, Tt, H, LV)
            A = -jnp.exp(A_log)
            dt = jax.nn.softplus(x @ Wdt.T + dt_bias)
            g = A[None, None, :] * dt
            Lam = jax.nn.softplus(Lp[None, None] * dl)
            cg = jnp.cumsum(g, axis=1)
            diff = cg[:, :, None, :] - cg[:, None, :, :]
            tri = np.tril(np.ones((Tt, Tt), dtype=bool))
            decay = jnp.exp(jnp.where(tri[None, :, :, None], diff, NEG))
            levels = _level_matrix(Tt, LV)
            lam_ts = jnp.take_along_axis(Lam[:, :, :, None, :], levels[None, :, None, :, None], axis=-1)[..., 0]
            scores = jnp.einsum('bthd,bshd->bhts', Q, K) * S ** (-0.5)
            Wmat = scores * jnp.transpose(decay, (0, 3, 1, 2)) * jnp.transpose(lam_ts, (0, 2, 1, 3))
            Y = jnp.einsum('bhts,bshd->bthd', Wmat, V).reshape(Bb, Tt, H * HD)
            o = Y @ Wout.T + x
            mu = o.mean(-1, keepdims=True)
            var = ((o - mu) ** 2).mean(-1, keepdims=True)
            return (o - mu) * jax.lax.rsqrt(var + 1e-05) * ln_g + ln_b
        return _forward(x, Wq, Wk, Wv, Wdl, Wdt, Wout, A_log, dt_bias, Lp, ln_g, ln_b)

    def _L0_ffn_ref(x, wf, uf, bf, wi, ui, bi, wc, uc, bc, wo, uo, bo, in_c):
        import jax, jax.numpy as jnp
        import numpy as np
        from jax import lax
        T, B, I, M, O = (64, 64, 256, 256, 256)

        def _xavier(key, shape):
            fan_out, fan_in = shape
            limit = float(np.sqrt(6.0 / (fan_in + fan_out)))
            return jax.random.uniform(key, shape, jnp.float32, -limit, limit)
        batch = x.shape[1]
        c0 = jnp.broadcast_to(in_c, (batch, in_c.shape[0]))

        def step(c, xt):
            ft = jax.nn.sigmoid(xt @ wf.T + c @ uf.T + bf)
            it = jax.nn.sigmoid(xt @ wi.T + c @ ui.T + bi)
            gt = jnp.tanh(xt @ wc.T + c @ uc.T + bc)
            c = ft * c + it * gt
            return (c, None)
        c_final, _ = lax.scan(step, c0, x)
        h = jnp.tanh(jnp.einsum('tbi,oi->tbo', x, wo) + c_final @ uo.T + bo)
        return h
    x = L0_attn_x
    x = _layernorm(x + _L0_attn_ref(x, L0_attn_Wq, L0_attn_Wk, L0_attn_Wv, L0_attn_Wdl, L0_attn_Wdt, L0_attn_Wout, L0_attn_A_log, L0_attn_dt_bias, L0_attn_Lp, L0_attn_ln_g, L0_attn_ln_b), axis=-1)
    x = _layernorm(x + _L0_ffn_ref(x, L0_ffn_wf, L0_ffn_uf, L0_ffn_bf, L0_ffn_wi, L0_ffn_ui, L0_ffn_bi, L0_ffn_wc, L0_ffn_uc, L0_ffn_bc, L0_ffn_wo, L0_ffn_uo, L0_ffn_bo, L0_ffn_in_c), axis=-1)
    return x

_drawn_inputs = setup_inputs


def setup_inputs(seed=0):
    import zlib

    import numpy as np

    out = dict(_drawn_inputs(seed))
    spreads = {'L0_attn_Lp': (1.0, 0.2),
     'L0_attn_ln_g': (1.0, 0.2),
     'L0_attn_ln_b': (0.0, 0.1),
     'L0_ffn_bf': (0.0, 0.1),
     'L0_ffn_bi': (0.0, 0.1),
     'L0_ffn_bc': (0.0, 0.1),
     'L0_ffn_bo': (0.0, 0.1),
     'L0_ffn_in_c': (0.0, 0.1)}
    factors = {}
    for name, (base, spread) in spreads.items():
        noise = np.random.default_rng([zlib.crc32(name.encode()), seed]).standard_normal(out[name].shape)
        drawn = base * np.exp(spread * noise) if base else spread * noise
        out[name] = jnp.asarray(drawn.astype(out[name].dtype))
    for name, factor in factors.items():
        out[name] = (out[name] * factor).astype(out[name].dtype)
    return out
```

```python
import numpy as np
import concourse.bass as bass
from concourse import mybir
from contextlib import ExitStack

P = 128
F32 = mybir.dt.float32
ALU = mybir.AluOpType
ACT = mybir.ActivationFunctionType
AX = mybir.AxisListType
H = 16
LV = 12
NL = LV + 1
NT = 4096
NC = NT // P
CB = 16
NSG = NC // 2
NEG = -1.0e30
LN2_64 = 64.0 * float(np.log(2.0))
TINY = 2.0 ** -64
EPS = 1e-5

C_TRI, C_ONE, C_ID = 0, 128, 256
C_MC, C_MF, C_NC, C_NF, C_OWN, C_EPS = 384, 408, 488, 496, 512, 520
C_HALF, C_END = 521, 522
B_LP, B_BI, B_AL, B_G, B_B, B_BO = 0, 208, 416, 432, 688, 944
B_END = 1200


def heads_of(g):
    return [8 * (g // 2) + (g % 2) + 2 * i for i in range(4)]


class Engine:

    def __init__(self, name, sem):
        self.name, self.sem, self.count, self.todo, self.seen = name, sem, 0, [], {}

    def wait(self, *tokens):
        for sem, value in [t for t in tokens if t is not None]:
            if self.seen.get(sem.name, 0) < value:
                self.seen[sem.name] = value
                self.todo.append(lambda e, s=sem, v=value: e.wait_ge(s, v))

    def run(self, *instructions):
        for f in instructions[:-1]:
            self.todo.append(f)
        self.count += 1
        self.todo.append(lambda e, f=instructions[-1]: f(e).then_inc(self.sem, 1))
        return (self.sem, self.count)

    def replay(self, e):
        for f in self.todo:
            f(e)


def bc(ap, axis, n):
    shape = list(ap.shape)
    shape.insert(axis, n)
    return ap.unsqueeze(axis).broadcast_to(shape)


def program(nc, x, xT, wqk, wtok, wout, wffn, cst, bcv, fv, out):
    ctx = ExitStack()
    with ctx:
        def sb(name, shape, dt=F32):
            return ctx.enter_context(nc.sbuf_tensor(name, shape, dt))

        def sem(name):
            return ctx.enter_context(nc.semaphore(name))

        banks = [ctx.enter_context(nc.psum_tensor(f"bank{i}", [P, 512], F32)) for i in range(8)]
        QB, PB, XB, YB, MB = banks[0], banks[1:3], banks[3:5], banks[5], banks[6:8]

        xs = sb("xs", [P, NC, 256])
        xts = sb("xts", [P, 2, NT])
        wq = sb("wq", [P, 2, 2048])
        wt = sb("wt", [P, 2, 464])
        wo = sb("wo", [P, 2, 256])
        cs = sb("cs", [P, C_END])
        bv = sb("bv", [P, B_END])
        fvs = sb("fvs", [P, 8])
        QT = [sb(f"QT{i}", [P, 8, 256]) for i in range(2)]
        KT = [sb(f"KT{i}", [P, 8, 256]) for i in range(2)]
        Kt = sb("Kt", [P, 1024])
        V = [sb(f"V{i}", [P, 2, 256]) for i in range(2)]
        Vw = [sb(f"Vw{i}", [P, 2, 256]) for i in range(2)]
        pre = sb("pre", [P, 2, 208])
        t1 = sb("t1", [P, 2, 208])
        t2 = sb("t2", [P, 2, 208])
        t3 = sb("t3", [P, 2, 208])
        t4 = sb("t4", [P, 2, 208])
        t5 = sb("t5", [P, 2, 208])
        ll = sb("ll", [P, 2, 208])
        eA = sb("eA", [P, H])
        gg = sb("gg", [P, 2, H])
        cgt = sb("cgt", [P, 2, 2 * H])
        ncg = [sb(f"ncg{i}", [P, 2, H]) for i in range(2)]
        dcol = sb("dcol", [P, 2, H])
        dv = sb("dv", [P, 2, H])
        dec = [sb(f"dec{i}", [P, 2, 8]) for i in range(2)]
        coef = [sb(f"coef{i}", [P, 2, H, 4]) for i in range(2)]
        lfp = sb("lfp", [P, 1280])
        lcp = sb("lcp", [P, 384])
        Lf = [sb(f"Lf{i}", [P, H, 16]) for i in range(2)]
        Lc = [sb(f"Lc{i}", [P, H, 8]) for i in range(2)]
        X = [sb(f"X{i}", [P, 512]) for i in range(2)]
        E = [sb(f"E{i}", [P, 512]) for i in range(2)]
        W = [sb(f"W{i}", [P, 512]) for i in range(2)]
        S = sb("S", [P, 8, 4, 16])
        zt = sb("zt", [P, 1024])
        zr = sb("zr", [P, 256])
        yf = sb("yf", [P, 256])
        yt = sb("yt", [P, 256])
        oo = sb("oo", [P, 256])
        nn = sb("nn", [P, 256])
        x1 = sb("x1", [P, 256])
        st1 = sb("st1", [P, 6])
        mv1 = sb("mv1", [P, 2])
        lr1 = sb("lr1", [P, 1])
        rs1 = sb("rs1", [P, 1])
        st2 = sb("st2", [P, 6])
        mv2 = sb("mv2", [P, 2])
        lr2 = sb("lr2", [P, 1])
        rs2 = sb("rs2", [P, 1])

        ident = cs[:, C_ID:C_ID + 128]

        PE = Engine("tensor", sem("s_pe"))
        DV = Engine("vector", sem("s_dve"))
        AC = Engine("scalar", sem("s_act"))
        GP = Engine("gpsimd", sem("s_pool"))
        SY = Engine("sync", sem("s_sync"))

        def load(name, *pairs):
            s = sem(name)
            for o, i in pairs:
                SY.todo.append(lambda e, o=o, i=i: e.dma_start(o, i).then_inc(s, 16))
            return (s, 16 * len(pairs))

        def kt(ap):
            return ap.rearrange("(k p) n -> p k n", p=P)

        l_cst = load("l_cst", (cs[:, :], cst), (bv[:, :], bcv), (fvs[:, :], fv))
        l_wt = load("l_wt", (wt[:, :, :], kt(wtok)))
        xv = x.rearrange("(n p) d -> p n d", p=P)
        l_x = []

        def load_x(sg):
            a, b = 256 * sg, 256 * sg + 256
            l_x.append(load(f"l_x{sg}", (xts[:, :, a:b], kt(xT)[:, :, a:b]),
                            (xs[:, 2 * sg:2 * sg + 2, :], xv[:, 2 * sg:2 * sg + 2, :])))

        load_x(0)
        l_wq = load("l_wq", (wq[:, :, :], kt(wqk)))
        load_x(1)
        l_wo = load("l_wo", (wo[:, :, :], kt(wout)))
        for sg in range(2, NSG):
            load_x(sg)

        T = {}
        free = {"Q": None, 0: None, 1: None}
        turn = [0]

        def misc():
            m = turn[0] % 2
            turn[0] += 1
            PE.wait(free[m])
            return m, MB[m]

        def mm(o, a, b, start=True, stop=True):
            return lambda e: e.matmul(o, a, b, start=start, stop=stop)

        def tr(o, i):
            return lambda e: e.transpose(o, i, ident)

        def act(o, i, f, **kw):
            return lambda e: e.activation(o, i, f, **kw)

        def tt(o, a, b, op):
            return lambda e: e.tensor_tensor(o, a, b, op)

        def ts(o, a, s1, s2, op0, op1=None):
            if op1 is None:
                return lambda e: e.tensor_scalar(o, a, s1, None, op0)
            return lambda e: e.tensor_scalar(o, a, s1, s2, op0, op1)

        def stt(o, a, s, b, op0, op1):
            return lambda e: e.scalar_tensor_tensor(out=o, in0=a, scalar=s, in1=b, op0=op0, op1=op1)

        def cp(o, i):
            return lambda e: e.tensor_copy(o, i)

        AC.todo.append(lambda e: e.preload_act_table_set("natural_log_exp_and_others"))
        AC.wait(l_cst)
        T["eA"] = AC.run(act(eA[:, :], bv[:, B_AL:B_AL + H], ACT.Exp))

        def project(sg, j):
            b = sg % 2
            q = j % 2 == 0
            m0 = j if q else 8 + j - 1
            PE.wait(l_x[sg], l_wq, free["Q"])
            ins = []
            for i in range(2):
                for k in range(2):
                    ins.append(mm(QB[:, 256 * i:256 * i + 256], wq[:, k, 128 * (m0 + i):128 * (m0 + i) + 128],
                                  xts[:, k, 256 * sg:256 * sg + 256], start=(k == 0), stop=(k == 1)))
            done = PE.run(*ins)
            src = QB[:, :].rearrange("p (m t) -> p m t", m=2)
            if q:
                AC.wait(done, T.get(("heads", sg - 2)))
                free["Q"] = AC.run(act(QT[b][:, m0:m0 + 2, :], src, ACT.Copy, scale=0.125))
                T["QT", sg, j] = free["Q"]
            else:
                DV.wait(done, T.get(("heads", sg - 2)))
                free["Q"] = DV.run(cp(KT[b][:, m0 - 8:m0 - 6, :], src))
                T["KT", sg, j] = free["Q"]

        def tokens(sg, j):
            b = sg % 2
            if j == 0:
                for c in range(2):
                    t = 256 * sg + 128 * c
                    PE.wait(l_x[sg], l_wt)
                    m, B = misc()
                    done = PE.run(*[mm(B[:, 0:464], xts[:, k, t:t + 128], wt[:, k, :], start=(k == 0), stop=(k == 1))
                                    for k in range(2)])
                    DV.wait(done, l_cst, T.get(("wv", sg - 2)), T.get("ll_used"))
                    DV.run(cp(V[b][:, c, :], B[:, 0:256]))
                    free[m] = DV.run(tt(pre[:, c, :], B[:, 256:464], bv[:, B_LP:B_LP + 208], ALU.mult))
                T["V", sg] = T["pre"] = free[m]
            if j == 1:
                DV.wait(T["pre"])
                a = DV.run(tt(pre[:, :, :], pre[:, :, :], bc(bv[:, B_BI:B_BI + 208], 1, 2), ALU.add))
                DV.wait(a)
                a = DV.run(stt(t1[:, :, :], pre[:, :, :], -1.0, pre[:, :, :], ALU.mult, ALU.max))
                AC.wait(a)
                a = AC.run(act(t2[:, :, :], t1[:, :, :], ACT.Exp, scale=-1.0))
                T["u"] = a
                AC.wait(a)
                T["lw"] = AC.run(act(t3[:, :, :], t2[:, :, :], ACT.Ln, bias=1.0))
            if j == 2:
                DV.wait(T["u"])
                a = DV.run(ts(t1[:, :, :], t2[:, :, :], 1.0, None, ALU.add))
                DV.wait(a)
                a = DV.run(lambda e: e.reciprocal(t4[:, :, :], t1[:, :, :]))
                b1 = DV.run(stt(t5[:, :, :], t1[:, :, :], -1.0, t2[:, :, :], ALU.add, ALU.subtract))
                DV.wait(b1, T["lw"])
                a = DV.run(tt(t4[:, :, :], t4[:, :, :], t5[:, :, :], ALU.mult))
                DV.wait(a)
                a = DV.run(tt(t3[:, :, :], t3[:, :, :], t4[:, :, :], ALU.subtract))
                DV.wait(a)
                T["sp"] = DV.run(stt(t3[:, :, :], pre[:, :, :], 0.0, t3[:, :, :], ALU.max, ALU.add))
            if j == 3:
                sp4 = t3[:, :, :].rearrange("p c (h l) -> p c h l", l=NL)
                DV.wait(T["sp"], T["eA"])
                a = DV.run(stt(gg[:, :, :], sp4[:, :, :, LV], -1.0, bc(eA[:, :], 1, 2), ALU.mult, ALU.mult))
                b1 = DV.run(ts(t1[:, :, :], t3[:, :, :], TINY, None, ALU.max))
                T["xm"] = DV.run(ts(t4[:, :, :], pre[:, :, :], LN2_64, 0.0, ALU.add, ALU.min))
                m, B = misc()
                PE.wait(a, l_cst)
                done = PE.run(
                    mm(B[:, 0:32], cs[:, C_TRI:C_TRI + 128], gg[:, :, :].rearrange("p c h -> p (c h)")),
                    mm(B[:, 32:64], cs[:, C_ONE:C_ONE + 128], gg[:, :, :].rearrange("p c h -> p (c h)")))
                AC.wait(b1)
                T["ln"] = AC.run(act(t2[:, :, :], t1[:, :, :], ACT.Ln))
                DV.wait(done, T.get("cgt_used"))
                free[m] = T["cgt"] = DV.run(cp(cgt[:, :, :].rearrange("p a n -> p (a n)"), B[:, 0:64]))
            if j == 4:
                cg = cgt[:, 0, :].rearrange("p (c h) -> p c h", c=2)
                tot = cgt[:, 1, :].rearrange("p (c h) -> p c h", c=2)
                DV.wait(T["cgt"], T["ln"], T.get(("exp", sg - 2)), T.get("dcol_used"))
                T["ncg", sg] = DV.run(ts(ncg[b][:, :, :], cg, -1.0, None, ALU.mult))
                a1 = DV.run(tt(dcol[:, :, :], tot, cg, ALU.subtract))
                a = DV.run(tt(t2[:, :, :], t2[:, :, :], t4[:, :, :], ALU.add))
                DV.wait(a)
                cgc = cgt[:, 0, :]
                T["ll"] = DV.run(tt(ll[:, :, :].rearrange("p c (h l) -> p (c h) l", l=NL),
                                    t2[:, :, :].rearrange("p c (h l) -> p (c h) l", l=NL),
                                    bc(cgc, 2, NL), ALU.add))
                AC.wait(a1, T["cgt"], T["ll"], T.get(("state", sg - 2)), T.get(("inter", sg - 2)), T.get("dv_used"))
                a = AC.run(act(dv[:, :, :], dcol[:, :, :], ACT.Exp))
                T["dcol_used"] = T["dv"] = a
                AC.run(act(dec[b][0:64, :, :], cgt[0:64, 1, :].rearrange("p (c q e) -> p c q e", c=2, e=2)[:, :, :, 0],
                           ACT.Exp))
                T["dec", sg] = T["cgt_used"] = AC.run(
                    act(dec[b][64:128, :, :], cgt[64:128, 1, :].rearrange("p (c q e) -> p c q e", c=2, e=2)[:, :, :, 1],
                        ACT.Exp))
                T["coef", sg] = AC.run(
                    act(coef[b][:, :, :, :].rearrange("p c h b -> p (c h) b"),
                        ll[:, :, :].rearrange("p c (h l) -> p (c h) l", l=NL)[:, :, 8:12], ACT.Exp))
            if j in (5, 7):
                c = (j - 5) // 2
                l3 = ll[:, c, :].rearrange("p (h l) -> p h l", l=NL)
                GP.wait(T["ll"], l_cst, T.get("red"))
                a = GP.run(tt(lfp[:, :].rearrange("p (h s l) -> p h s l", h=H, s=16), bc(l3[:, :, 0:5], 2, 16),
                              bc(cs[:, C_MF:C_MF + 80].rearrange("p (s l) -> p s l", l=5), 1, H), ALU.mult))
                b1 = GP.run(tt(lcp[:, :].rearrange("p (h s l) -> p h s l", h=H, s=8), bc(l3[:, :, 5:8], 2, 8),
                               bc(cs[:, C_MC:C_MC + 24].rearrange("p (s l) -> p s l", l=3), 1, H), ALU.mult))
                T["prod"] = (a, b1)
                if c == 1:
                    T["ll_used"] = b1
                DV.wait(a, b1, T.get(("xbuilt", 2 * sg + c - 2)))
                a = DV.run(lambda e: e.tensor_reduce(Lf[c][:, :, :], lfp[:, :].rearrange("p (h s l) -> p h s l", h=H, s=16),
                                                     AX.X, ALU.add))
                b1 = DV.run(lambda e: e.tensor_reduce(Lc[c][:, :, :], lcp[:, :].rearrange("p (h s l) -> p h s l", h=H, s=8),
                                                      AX.X, ALU.add))
                T["red"] = b1
                DV.wait(a, b1)
                DV.run(tt(Lf[c][:, :, :], Lf[c][:, :, :], bc(cs[:, C_NF:C_NF + 16], 1, H), ALU.add))
                T["L", 2 * sg + c] = DV.run(tt(Lc[c][:, :, :], Lc[c][:, :, :], bc(cs[:, C_NC:C_NC + 8], 1, H), ALU.add))
            if j == 5:
                DV.wait(T["dv"], T["V", sg], T.get(("state", sg - 2)))
                T["Vw", sg] = T["dv_used"] = DV.run(
                    tt(Vw[b][:, :, :].rearrange("p c (h d) -> p (c h) d", h=H),
                       V[b][:, :, :].rearrange("p c (h d) -> p (c h) d", h=H),
                       bc(dv[:, :, :].rearrange("p c h -> p (c h)"), 2, 16), ALU.mult))

        def exponents(G):
            ci, g = G // 4, G % 4
            c, h0, i = ci % 2, heads_of(G % 4)[0], G % 2
            x4 = X[i][:, :].rearrange("p (h b s) -> p h b s", h=4, b=8)
            GP.wait(T["L", ci], T.get(("xt", G - 2)))
            a = GP.run(tt(x4, bc(Lf[c][:, h0:h0 + 7:2, :], 2, 8),
                          cs[:, C_OWN:C_OWN + 8].unsqueeze(1).unsqueeze(3).broadcast_to([P, 4, 8, 16]), ALU.mult))
            GP.wait(a)
            T["x", G] = GP.run(tt(x4, x4, bc(Lc[c][:, h0:h0 + 7:2, :], 3, 16), ALU.add))
            if g == 3:
                T["xbuilt", ci] = T["x", G]

        def qk_ready(sg):
            return [T["QT", sg, 6], T["KT", sg, 7]]

        def scores(G):
            ci, g, i = G // 4, G % 4, G % 2
            sg, c, b = ci // 2, ci % 2, (ci // 2) % 2
            hs = heads_of(g)
            r = 64 * (hs[0] % 2)
            PE.wait(T.get(("w", G - 2)), *qk_ready(sg))
            T["p", G] = PE.run(*[
                mm(PB[i][:, 128 * n:128 * n + 128], KT[b][r:r + 64, h // 2, 128 * c:128 * c + 128],
                   QT[b][r:r + 64, h // 2, 128 * c:128 * c + 128]) for n, h in enumerate(hs)])
            PE.wait(T["x", G], T.get(("e", G - 2)))
            T["xt", G] = PE.run(*[tr(XB[i][:, 128 * n:128 * n + 128], X[i][:, 128 * n:128 * n + 128])
                                  for n in range(4)])
            AC.wait(T["xt", G], T["ncg", sg], T.get(("w", G - 2)))
            T["e", G] = AC.run(*[act(E[i][:, 128 * n:128 * n + 128], XB[i][:, 128 * n:128 * n + 128], ACT.Exp,
                                     bias=ncg[b][:, c, h:h + 1]) for n, h in enumerate(hs)])
            if c == 1 and g == 3:
                T["exp", sg] = T["e", G]
            DV.wait(T["p", G], T["e", G], T.get(("y", G - 2)))
            T["w", G] = DV.run(tt(W[i][:, :], PB[i][:, :], E[i][:, :], ALU.mult))

        def weigh(G):
            ci, g, i = G // 4, G % 4, G % 2
            sg, c, b = ci // 2, ci % 2, (ci // 2) % 2
            PE.wait(T["w", G], T["V", sg])
            if g == 0:
                PE.wait(T.get(("yf", ci - 1)))
            T["y", G] = PE.run(*[mm(YB[:, 16 * h:16 * h + 16], W[i][:, 128 * n:128 * n + 128],
                                    V[b][:, c, 16 * h:16 * h + 16]) for n, h in enumerate(heads_of(g))])
            if c == 1 and g == 3:
                T["wv", sg] = T["y", G]

        def keys(ci):
            sg, c, b = ci // 2, ci % 2, (ci // 2) % 2
            PE.wait(*qk_ready(sg))
            for n in range(2):
                m, B = misc()
                done = PE.run(*[tr(B[:, 128 * q:128 * q + 128], KT[b][:, 4 * n + q, 128 * c:128 * c + 128])
                                for q in range(4)])
                AC.wait(done, T.get("kt_used"))
                free[m] = AC.run(act(Kt[:, 512 * n:512 * n + 512], B[:, :], ACT.Copy))
            T["kt"] = free[m]

        def inter(ci):
            cc = ci % CB
            sg, c, b = ci // 2, ci % 2, (ci // 2) % 2
            nb = cc.bit_length()
            if nb == 0:
                return
            zs = []
            for e2 in range(2):
                m, B = misc()
                r = 64 * e2
                PE.wait(T["S"])
                done = PE.run(*[mm(B[:, 64 * p:64 * p + 16 * nb], QT[b][r:r + 64, p, 128 * c:128 * c + 128],
                                   S[r:r + 64, p, 0:nb, :].rearrange("p b d -> p (b d)")) for p in range(8)])
                DV.wait(done, T["coef", sg], T.get("zr_done"))
                zv = zt[:, 0:8 * 2 * nb * 16].rearrange("p (q e n) -> p q e n", q=8, e=2)[:, :, e2, :]
                zv = zv.rearrange("p q (b d) -> p q b d", d=16)
                free[m] = DV.run(tt(zv, B[:, :].rearrange("p (q b d) -> p q b d", q=8, d=16)[:, :, 0:nb, :],
                                    bc(coef[b][:, c, e2:16:2, 0:nb], 3, 16), ALU.mult))
                zs.append(free[m])
            T["S_read"] = done
            if c == 1:
                T["inter", sg] = free[m]
            DV.wait(*zs, T.get(("yf", ci - 1)))
            T["zr"] = T["zr_done"] = DV.run(lambda e: e.tensor_reduce(
                zr[:, :].rearrange("p (h d) -> p h d", d=16),
                zt[:, 0:16 * nb * 16].rearrange("p (h b d) -> p h d b", h=H, d=16), AX.X, ALU.add))

        def state(ci):
            cc = ci % CB
            sg, c, b = ci // 2, ci % 2, (ci // 2) % 2
            if cc < CB - 1:
                nb, z = cc.bit_length(), ((cc + 1) & -(cc + 1)).bit_length() - 1
                m, B = misc()
                PE.wait(T["kt"], T["Vw", sg])
                done = PE.run(*[mm(B[:, 32 * p:32 * p + 32], Kt[:, 128 * p:128 * p + 128],
                                   Vw[b][:, c, 32 * p:32 * p + 32]) for p in range(8)])
                T["kt_used"] = done
                DV.wait(T["dec", sg], T.get("S_read"), T.get("S"))
                a = None
                if nb:
                    s3 = S[:, :, 0:nb, :].rearrange("p q b d -> p q (b d)")
                    a = DV.run(tt(s3, s3, bc(dec[b][:, c, :], 2, 16 * nb), ALU.mult))
                DV.wait(done, a)
                for e2 in range(2):
                    r = slice(64 * e2, 64 * e2 + 64)
                    src = B[r, 0:256].rearrange("p (q n) -> p q n", q=8)[:, :, 16 * e2:16 * e2 + 16]
                    if z == 0:
                        a = DV.run(cp(S[r, :, 0, :], src))
                    else:
                        a = DV.run(tt(S[r, :, z, :], src, S[r, :, 0, :], ALU.add))
                free[m] = a
                for l in range(1, z):
                    DV.wait(a)
                    a = DV.run(tt(S[:, :, z, :], S[:, :, z, :], S[:, :, l, :], ALU.add))
                if z:
                    DV.wait(a)
                    a = DV.run(lambda e: e.memset(S[:, :, 0:z, :], 0.0))
                T["S"] = a
                if c == 1:
                    T["state", sg] = a
            elif c == 1:
                T["state", sg] = T["S"]

        def gather(ci):
            cc = ci % CB
            DV.wait(T["y", 4 * ci + 3], T.get("yt_done"))
            if cc:
                DV.wait(T["zr"])
                T["yf", ci] = DV.run(tt(yf[:, :], YB[:, 0:256], zr[:, :], ALU.add))
            else:
                T["yf", ci] = DV.run(cp(yf[:, :], YB[:, 0:256]))

        def turn_y(ci):
            m, B = misc()
            PE.wait(T["yf", ci])
            done = PE.run(*[tr(B[:, 128 * k:128 * k + 128], yf[:, 128 * k:128 * k + 128]) for k in range(2)])
            T["yt_done"] = done
            AC.wait(done, T.get("op_done"))
            free[m] = T["yt"] = AC.run(act(yt[:, :], B[:, 0:256], ACT.Copy))

        def norm(o, i, st, mv, lr, rs, key, used):
            a = DV.run(lambda e: e.bn_stats(st[:, :], i))
            DV.wait(a, used)
            a = DV.run(lambda e: e.bn_aggr(mv[:, :], st[:, :]))
            GP.wait(a, l_cst)
            a = GP.run(tt(lr[:, :], mv[:, 1:2], cs[:, C_EPS:C_EPS + 1], ALU.add))
            GP.wait(a)
            T[key] = GP.run(tt(rs[:, :], lr[:, :], cs[:, C_HALF:C_HALF + 1], ALU.pow))

        def out_proj(ci):
            m, B = misc()
            PE.wait(T["yt"], l_wo)
            done = PE.run(*[mm(B[:, 0:256], yt[:, 128 * k:128 * k + 128], wo[:, k, :], start=(k == 0), stop=(k == 1))
                            for k in range(2)])
            T["op_done"] = done
            DV.wait(done, l_x[ci // 2])
            free[m] = DV.run(tt(oo[:, :], B[:, 0:256], xs[:, ci, :], ALU.add))
            DV.wait(free[m])
            norm(None, oo[:, :], st1, mv1, lr1, rs1, "rs1", None)

        def normalise(ci):
            DV.wait(T["rs1"], T.get("nn_used"))
            a = DV.run(ts(nn[:, :], oo[:, :], mv1[:, 0:1], rs1[:, 0:1], ALU.subtract, ALU.mult))
            GP.wait(a, l_x[ci // 2], T.get("x1_used"))
            a = GP.run(tt(nn[:, :], nn[:, :], bv[:, B_G:B_G + 256], ALU.mult))
            GP.wait(a)
            a = GP.run(tt(nn[:, :], nn[:, :], bv[:, B_B:B_B + 256], ALU.add))
            GP.wait(a)
            T["x1"] = T["nn_used"] = GP.run(tt(x1[:, :], nn[:, :], xs[:, ci, :], ALU.add))

        def outer_stats(ci):
            DV.wait(T["x1"])
            norm(None, x1[:, :], st2, mv2, lr2, rs2, "rs2", None)

        def outer_norm(ci):
            DV.wait(T["rs2"])
            T["x2", ci] = T["x1_used"] = DV.run(
                ts(xs[:, ci, :], x1[:, :], mv2[:, 0:1], rs2[:, 0:1], ALU.subtract, ALU.mult))

        def turn_x(ci):
            m, B = misc()
            PE.wait(T["x2", ci])
            done = PE.run(*[tr(B[:, 128 * k:128 * k + 128], xs[:, ci, 128 * k:128 * k + 128]) for k in range(2)])
            AC.wait(done)
            free[m] = T["x2t", ci] = AC.run(act(xts[:, :, 128 * ci:128 * ci + 128],
                                                B[:, 0:256].rearrange("p (k t) -> p k t", k=2), ACT.Copy))

        tail = {4: gather, 6: turn_y, 7: out_proj, 8: normalise, 9: outer_stats, 10: outer_norm, 11: turn_x}
        for s in range(-8, 4 * NC + 12):
            sg, j = (s + 8) // 8, (s + 8) % 8
            if sg < NSG:
                project(sg, j)
            if 0 <= s < 4 * NC:
                scores(s)
            if 0 <= s < 4 * NC and s % 4 < 3:
                [keys, inter, state][s % 4](s // 4)
            if 0 <= s - 1 < 4 * NC:
                weigh(s - 1)
            if sg < NSG:
                tokens(sg, j)
            if 0 <= s + 1 < 4 * NC:
                exponents(s + 1)
            if 0 < s < 4 * NC and s % 8 == 7:
                T["heads", s // 8] = T["kt_used"] if T["kt_used"][1] > T["p", s][1] else T["p", s]
            for d, f in tail.items():
                if s - d >= 0 and (s - d) % 4 == 0 and (s - d) // 4 < NC:
                    f((s - d) // 4)

        w = wq[:, :, :].rearrange("p k (w n) -> p k w n", w=8)
        s_wf = sem("l_wf")
        SY.wait(T["heads", NSG - 1])
        SY.todo.append(lambda e: e.dma_start(w, wffn.rearrange("(k p) w n -> p k w n", p=P)).then_inc(s_wf, 16))
        l_wf = (s_wf, 16)
        WF, WI, WC, UF, UI, UC, WO, UO = range(8)
        b0 = sb("b0", [P, 2, 3])
        gb = [[QT[i][:, 2 * n:2 * n + 2, :].rearrange("p m t -> p (m t)") for n in range(3)] for i in range(2)]
        cells = [KT[i][:, :, :].rearrange("p (c k u) t -> p c k (u t)", c=2, k=2) for i in range(2)]
        c1 = [cells[0][:, i, :, :] for i in range(2)]
        c2 = [cells[1][:, i, :, :] for i in range(2)]
        cu = [sb(f"cu{i}", [P, 256]) for i in range(2)]
        hh = [sb(f"hh{i}", [P, 512]) for i in range(2)]
        st3 = sb("st3", [P, 4, 6])
        mv3 = sb("mv3", [P, NC, 2])
        rs3 = sb("rs3", [P, NC])
        lr3 = sb("lr3", [P, NC])
        ring = [banks[0:3], banks[3:6]]
        bank_free = [[free["Q"], T["w", 4 * NC - 2], T["w", 4 * NC - 1]],
                     [T["e", 4 * NC - 2], T["e", 4 * NC - 1], T["yf", NC - 1]]]
        c0 = fvs[:, 6:8]
        m, B = misc()
        PE.wait(l_wf)
        ins = []
        for mt in range(2):
            for n in range(3):
                for k in range(2):
                    ins.append(mm(B[:, 3 * mt + n:3 * mt + n + 1], w[:, k, UF + n, 128 * mt:128 * mt + 128],
                                  c0[:, k:k + 1], start=(k == 0), stop=(k == 1)))
        done = PE.run(*ins)
        DV.wait(done)
        free[m] = T["b0"] = DV.run(tt(b0[:, :, :].rearrange("p m n -> p (m n)"), B[:, 0:6], fvs[:, 0:6], ALU.add))
        cell = [0]

        def gates(blk, t):
            a0 = 2048 * t + 512 * blk
            for mt in range(2):
                i = cell[0] % 2
                cell[0] += 1
                res = []
                for n in range(3):
                    PE.wait(bank_free[i][n], *[T["x2t", 16 * t + 4 * blk + q] for q in range(4)])
                    ops = [(w[:, k, WF + n, 128 * mt:128 * mt + 128], xts[:, k, a0:a0 + 512]) for k in range(2)]
                    if t:
                        PE.wait(T["c1", blk])
                        ops += [(w[:, k, UF + n, 128 * mt:128 * mt + 128], c1[blk % 2][:, k, :]) for k in range(2)]
                    done = PE.run(*[mm(ring[i][n][:, :], l, r, start=(q == 0), stop=(q == len(ops) - 1))
                                    for q, (l, r) in enumerate(ops)])
                    AC.wait(done, T["b0"], T.get(("cell", i)))
                    bias = fvs[:, 3 * mt + n:3 * mt + n + 1] if t else b0[:, mt, n:n + 1]
                    bank_free[i][n] = AC.run(act(gb[i][n], ring[i][n][:, :], ACT.Tanh if n == 2 else ACT.Sigmoid,
                                                 bias=bias))
                    res.append(bank_free[i][n])
                DV.wait(*res)
                a = DV.run(tt(gb[i][1], gb[i][1], gb[i][2], ALU.mult))
                if t == 0:
                    DV.wait(a, T.get(("gates1", blk - 2)))
                    T["cell", i] = DV.run(stt(c1[blk % 2][:, mt, :], gb[i][0], c0[:, mt:mt + 1], gb[i][1],
                                              ALU.mult, ALU.add))
                else:
                    a1 = DV.run(tt(gb[i][0], gb[i][0], c1[blk % 2][:, mt, :], ALU.mult))
                    DV.wait(a, a1, T.get(("out", blk - 2)))
                    T["cell", i] = DV.run(tt(c2[blk % 2][:, mt, :], gb[i][0], gb[i][1], ALU.add))
            if t == 0:
                T["c1", blk] = T["cell", i]
            else:
                T["gates1", blk] = done
                T["c2", blk] = T["cell", i]

        def outputs(blk):
            for q in range(4):
                tt_ = 4 * blk + q
                i = tt_ % 2
                cT = c2[blk % 2]
                m, B = misc()
                PE.wait(T["c2", blk])
                done = PE.run(*[mm(B[:, 0:256], cT[:, k, 128 * q:128 * q + 128], w[:, k, UO, :],
                                   start=(k == 0), stop=(k == 1)) for k in range(2)])
                DV.wait(done, T.get(("cu", i)))
                free[m] = a0 = DV.run(tt(cu[i][:, :], B[:, 0:256], bv[:, B_BO:B_BO + 256], ALU.add))
                m, B = misc()
                done = PE.run(*[mm(B[:, 256 * t:256 * t + 256], xts[:, k, 2048 * t + 128 * tt_:2048 * t + 128 * tt_ + 128],
                                   w[:, k, WO, :], start=(k == 0), stop=(k == 1)) for t in range(2) for k in range(2)])
                h3 = hh[i][:, :].rearrange("p (t n) -> p t n", t=2)
                DV.wait(done, a0, T.get(("hh", i)))
                free[m] = T["cu", i] = DV.run(tt(h3, B[:, :].rearrange("p (t n) -> p t n", t=2), bc(cu[i][:, :], 1, 2),
                                                 ALU.add))
                AC.wait(free[m])
                a = AC.run(act(hh[i][:, :], hh[i][:, :], ACT.Tanh))
                GP.wait(a)
                dst = xs[:, tt_:tt_ + 17:16, :]
                T["hh", i] = a = GP.run(tt(dst, dst, h3, ALU.add))
                DV.wait(a)
                s2 = [DV.run(lambda e, t=t, i=i, tt_=tt_: e.bn_stats(st3[:, 2 * i + t, :], xs[:, tt_ + 16 * t, :])) for t in range(2)]
                DV.wait(*s2)
                for t in range(2):
                    a = DV.run(lambda e, t=t, i=i, tt_=tt_: e.bn_aggr(mv3[:, tt_ + 16 * t, :], st3[:, 2 * i + t, :]))
                T["mv3", tt_] = a
            T["out", blk] = done

        for blk in range(4):
            gates(blk, 0)
            gates(blk, 1)
            if blk:
                outputs(blk - 1)
        outputs(3)
        GP.wait(T["mv3", 15])
        a = GP.run(tt(lr3[:, :], mv3[:, :, 1], cs[:, C_EPS:C_EPS + 1].broadcast_to([P, NC]), ALU.add))
        GP.wait(a)
        a = GP.run(tt(rs3[:, :], lr3[:, :], cs[:, C_HALF:C_HALF + 1].broadcast_to([P, NC]), ALU.pow))
        DV.wait(a)
        ov = out.rearrange("(n p) d -> p n d", p=P)
        s_out = sem("s_out")
        for n in range(NC):
            a = DV.run(ts(xs[:, n, :], xs[:, n, :], mv3[:, n, 0:1], rs3[:, n:n + 1], ALU.subtract, ALU.mult))
            if n % 2:
                SY.wait(a)
                SY.todo.append(lambda e, n=n: e.dma_start(ov[:, n - 1:n + 1, :], xs[:, n - 1:n + 1, :]).then_inc(s_out, 16))
        SY.wait((s_out, 16 * (NC // 2)))

        block = ctx.enter_context(nc.Block())

        @block.sync
        def _(e):
            SY.replay(e)

        @block.tensor
        def _(e):
            PE.replay(e)

        @block.vector
        def _(e):
            DV.replay(e)

        @block.scalar
        def _(e):
            AC.replay(e)

        @block.gpsimd
        def _(e):
            GP.replay(e)


def constants():
    c = np.zeros((P, C_END), np.float32)
    t = np.arange(P)
    c[:, C_TRI:C_TRI + 128] = t[:, None] <= t[None, :]
    c[:, C_ONE:C_ONE + 128] = 1.0
    c[:, C_ID:C_ID + 128] = np.eye(P)

    def level(a, b):
        v = a ^ b
        return int(v).bit_length()

    for p in range(P):
        for b in range(8):
            k = p // 16
            if b < k:
                c[p, C_MC + 3 * b + level(k, b) - 1] = 1.0
            if b > k:
                c[p, C_NC + b] = NEG
            if b == k:
                c[p, C_OWN + b] = 1.0
        for s in range(16):
            if s <= p % 16:
                c[p, C_MF + 5 * s + level(p % 16, s)] = 1.0
            else:
                c[p, C_NF + s] = NEG
    c[:, C_EPS] = EPS
    c[:, C_HALF] = -0.5
    return c


def kernel(**a):
    import concourse.bacc as bacc
    from concourse.bass_utils import run_bass_kernel_spmd

    a = {k: np.asarray(v) for k, v in a.items()}
    f = {k.replace("L0_attn_", "").replace("L0_ffn_", "f_"): v for k, v in a.items()}
    x = np.ascontiguousarray(f["x"].reshape(NT, 256))
    dlt = np.concatenate([f["Wdl"].reshape(H, LV, 256), f["Wdt"].reshape(H, 1, 256)], 1).reshape(H * NL, 256)
    lp = np.concatenate([f["Lp"], np.ones((H, 1), np.float32)], 1).reshape(-1)
    bi = np.concatenate([np.zeros((H, LV), np.float32), f["dt_bias"].reshape(H, 1)], 1).reshape(-1)
    row = np.concatenate([lp, bi, f["A_log"], f["ln_g"], f["ln_b"], f["f_bo"]])
    fv = np.concatenate([np.stack([f["f_bf"], f["f_bi"], f["f_bc"]], 1).reshape(2, P, 3).transpose(1, 0, 2).reshape(P, 6),
                         f["f_in_c"].reshape(2, P).T], 1)
    data = {
        "x": x,
        "xT": x.T,
        "wqk": np.concatenate([f["Wq"], f["Wk"]], 0).T,
        "wtok": np.concatenate([f["Wv"], dlt], 0).T,
        "wout": f["Wout"].T,
        "wffn": np.stack([f["f_" + n].T for n in ("wf", "wi", "wc", "uf", "ui", "uc", "wo", "uo")], 1),
        "cst": constants(),
        "bcv": np.broadcast_to(row, (P, B_END)),
        "fv": fv,
    }
    data = {k: np.ascontiguousarray(v) for k, v in data.items()}
    nc = bacc.Bacc("TRN2", target_bir_lowering=False, num_devices=1)
    aps = [nc.dram_tensor("in_" + k, v.shape, F32, kind="ExternalInput").ap() for k, v in data.items()]
    aps.append(nc.dram_tensor("out_0", (NT, 256), F32, kind="ExternalOutput").ap())
    program(nc, *aps)
    r = run_bass_kernel_spmd(nc, [{"in_" + k: v for k, v in data.items()}], core_ids=[0])
    return r.results[0]["out_0"].reshape(2, 2048, 256)
```

```python
import numpy as np
import concourse.bass as bass
from concourse import mybir
from contextlib import ExitStack

P = 128
F32 = mybir.dt.float32
ALU = mybir.AluOpType
ACT = mybir.ActivationFunctionType
AX = mybir.AxisListType
H = 16
LV = 12
NL = LV + 1
NT = 4096
NC = NT // P
CB = 16
NSG = NC // 2
NEG = -1.0e30
LN2_64 = 64.0 * float(np.log(2.0))
TINY = 2.0 ** -64
EPS = 1e-5

C_TRI, C_ONE, C_ID = 0, 128, 256
C_MC, C_MF, C_NC, C_NF, C_OWN, C_EPS = 384, 408, 488, 496, 512, 520
C_HALF, C_END = 521, 522
B_LP, B_BI, B_AL, B_G, B_B, B_BO = 0, 208, 416, 432, 688, 944
B_END = 1200


def heads_of(g):
    return [8 * (g // 2) + (g % 2) + 2 * i for i in range(4)]


class Engine:

    def __init__(self, name, sem):
        self.name, self.sem, self.count, self.todo, self.seen = name, sem, 0, [], {}

    def wait(self, *tokens):
        for sem, value in [t for t in tokens if t is not None]:
            if self.seen.get(sem.name, 0) < value:
                self.seen[sem.name] = value
                self.todo.append(lambda e, s=sem, v=value: e.wait_ge(s, v))

    def run(self, *instructions):
        for f in instructions[:-1]:
            self.todo.append(f)
        self.count += 1
        self.todo.append(lambda e, f=instructions[-1]: f(e).then_inc(self.sem, 1))
        return (self.sem, self.count)

    def weave(self, *jobs):
        most = max([len(ins) for _, ins in jobs] + [1])
        order = sorted(((n + 0.5) * most / len(ins), k, n) for k, (_, ins) in enumerate(jobs) for n in range(len(ins)))
        tokens = [None] * len(jobs)
        for _, k, n in order:
            waits, ins = jobs[k]
            if n == 0:
                self.wait(*waits)
            if n == len(ins) - 1:
                tokens[k] = self.run(ins[n])
            else:
                self.todo.append(ins[n])
        return tokens

    def replay(self, e):
        for f in self.todo:
            f(e)


def bc(ap, axis, n):
    shape = list(ap.shape)
    shape.insert(axis, n)
    return ap.unsqueeze(axis).broadcast_to(shape)


def program(nc, x, xT, wqk, wtok, wout, wffn, cst, bcv, fv, out):
    ctx = ExitStack()
    with ctx:
        def sb(name, shape, dt=F32):
            return ctx.enter_context(nc.sbuf_tensor(name, shape, dt))

        def sem(name):
            return ctx.enter_context(nc.semaphore(name))

        banks = [ctx.enter_context(nc.psum_tensor(f"bank{i}", [P, 512], F32)) for i in range(8)]
        QB, PB, XB, YB, MB = banks[0], banks[1:3], banks[3:5], banks[5], banks[6:8]

        xs = sb("xs", [P, NC, 256])
        xts = sb("xts", [P, 2, NT])
        wq = sb("wq", [P, 2, 2048])
        wt = sb("wt", [P, 2, 464])
        wo = sb("wo", [P, 2, 256])
        cs = sb("cs", [P, C_END])
        bv = sb("bv", [P, B_END])
        fvs = sb("fvs", [P, 8])
        QT = [sb(f"QT{i}", [P, 8, 256]) for i in range(2)]
        KT = [sb(f"KT{i}", [P, 8, 256]) for i in range(2)]
        Kt = sb("Kt", [P, 1024])
        V = [sb(f"V{i}", [P, 2, 256]) for i in range(3)]
        Vw = [sb(f"Vw{i}", [P, 2, 256]) for i in range(2)]
        pre = sb("pre", [P, 2, 208])
        t1 = sb("t1", [P, 2, 208])
        t2 = sb("t2", [P, 2, 208])
        t3 = sb("t3", [P, 2, 208])
        t4 = sb("t4", [P, 2, 208])
        t5 = sb("t5", [P, 2, 208])
        ll = sb("ll", [P, 2, 208])
        eA = sb("eA", [P, H])
        gg = sb("gg", [P, 2, H])
        cgt = sb("cgt", [P, 2, 2 * H])
        ncg = [sb(f"ncg{i}", [P, 2, H]) for i in range(2)]
        dcol = sb("dcol", [P, 2, H])
        dv = sb("dv", [P, 2, H])
        dec = [sb(f"dec{i}", [P, 2, 8]) for i in range(2)]
        coef = [sb(f"coef{i}", [P, 2, H, 4]) for i in range(2)]
        lfp = sb("lfp", [P, 1280])
        lcp = sb("lcp", [P, 384])
        Lf = [sb(f"Lf{i}", [P, H, 16]) for i in range(4)]
        Lc = [sb(f"Lc{i}", [P, H, 8]) for i in range(4)]
        X = [sb(f"X{i}", [P, 512]) for i in range(3)]
        E = [sb(f"E{i}", [P, 512]) for i in range(2)]
        W = [sb(f"W{i}", [P, 512]) for i in range(2)]
        S = sb("S", [P, 8, 4, 16])
        Sd = sb("Sd", [P, 8, 2, 64])
        zt = sb("zt", [P, 1024])
        zr = [sb(f"zr{i}", [P, 256]) for i in range(2)]
        yf = sb("yf", [P, 256])
        yt = sb("yt", [P, 256])
        oo = sb("oo", [P, 256])
        nn = sb("nn", [P, 256])
        x1 = sb("x1", [P, 256])
        st1 = sb("st1", [P, 6])
        mv1 = sb("mv1", [P, 2])
        lr1 = sb("lr1", [P, 1])
        rs1 = sb("rs1", [P, 1])
        st2 = sb("st2", [P, 6])
        mv2 = sb("mv2", [P, 2])
        lr2 = sb("lr2", [P, 1])
        rs2 = sb("rs2", [P, 1])

        ident = cs[:, C_ID:C_ID + 128]

        PE = Engine("tensor", sem("s_pe"))
        DV = Engine("vector", sem("s_dve"))
        AC = Engine("scalar", sem("s_act"))
        GP = Engine("gpsimd", sem("s_pool"))
        SY = Engine("sync", sem("s_sync"))

        def load(name, *pairs):
            s = sem(name)
            for o, i in pairs:
                SY.todo.append(lambda e, o=o, i=i: e.dma_start(o, i).then_inc(s, 16))
            return (s, 16 * len(pairs))

        def kt(ap):
            return ap.rearrange("(k p) n -> p k n", p=P)

        l_cst = load("l_cst", (cs[:, :], cst), (bv[:, :], bcv), (fvs[:, :], fv))
        l_wt = load("l_wt", (wt[:, :, :], kt(wtok)))
        xv = x.rearrange("(n p) d -> p n d", p=P)
        l_x = []

        def load_x(sg):
            a, b = 256 * sg, 256 * sg + 256
            l_x.append(load(f"l_x{sg}", (xts[:, :, a:b], kt(xT)[:, :, a:b]),
                            (xs[:, 2 * sg:2 * sg + 2, :], xv[:, 2 * sg:2 * sg + 2, :])))

        load_x(0)
        l_wq = load("l_wq", (wq[:, :, :], kt(wqk)))
        load_x(1)
        l_wo = load("l_wo", (wo[:, :, :], kt(wout)))
        for sg in range(2, NSG):
            load_x(sg)

        T = {}
        free = {"Q": None, 0: None, 1: None}
        turn = [0]

        def misc():
            m = turn[0] % 2
            turn[0] += 1
            return m, MB[m], free[m]

        def mm(o, a, b, start=True, stop=True):
            return lambda e: e.matmul(o, a, b, start=start, stop=stop)

        def tr(o, i):
            return lambda e: e.transpose(o, i, ident)

        def act(o, i, f, **kw):
            return lambda e: e.activation(o, i, f, **kw)

        def tt(o, a, b, op):
            return lambda e: e.tensor_tensor(o, a, b, op)

        def ts(o, a, s1, s2, op0, op1=None):
            if op1 is None:
                return lambda e: e.tensor_scalar(o, a, s1, None, op0)
            return lambda e: e.tensor_scalar(o, a, s1, s2, op0, op1)

        def stt(o, a, s, b, op0, op1):
            return lambda e: e.scalar_tensor_tensor(out=o, in0=a, scalar=s, in1=b, op0=op0, op1=op1)

        def cp(o, i):
            return lambda e: e.tensor_copy(o, i)

        T["Sd0"] = GP.run(lambda e: e.memset(Sd[:, :, :, :], 0.0))
        AC.todo.append(lambda e: e.preload_act_table_set("natural_log_exp_and_others"))
        AC.wait(l_cst)
        T["eA"] = AC.run(act(eA[:, :], bv[:, B_AL:B_AL + H], ACT.Exp))

        def project(sg, j):
            b = sg % 2
            q = j % 2 == 0
            m0 = j if q else 8 + j - 1
            waits = [l_x[sg], l_wq, free["Q"]]
            ins = []
            for i in range(2):
                for k in range(2):
                    ins.append(mm(QB[:, 256 * i:256 * i + 256], wq[:, k, 128 * (m0 + i):128 * (m0 + i) + 128],
                                  xts[:, k, 256 * sg:256 * sg + 256], start=(k == 0), stop=(k == 1)))
            done, = yield [(waits, ins)]
            src = QB[:, :].rearrange("p (m t) -> p m t", m=2)
            if q:
                AC.wait(done, T.get(("heads", sg - 2)))
                free["Q"] = AC.run(act(QT[b][:, m0:m0 + 2, :], src, ACT.Copy, scale=0.125))
                T["QT", sg, j] = free["Q"]
            else:
                DV.wait(done, T.get(("heads", sg - 2)))
                free["Q"] = DV.run(cp(KT[b][:, m0 - 8:m0 - 6, :], src))
                T["KT", sg, j] = free["Q"]

        def tokens(sg, j):
            b = sg % 2
            if j == 0:
                ms = [misc() for c in range(2)]
                dones = yield [([l_x[sg], l_wt, wb], [
                    mm(B[:, 0:464], xts[:, k, 256 * sg + 128 * c:256 * sg + 128 * c + 128], wt[:, k, :],
                       start=(k == 0), stop=(k == 1)) for k in range(2)]) for c, (m, B, wb) in enumerate(ms)]
                for c, ((m, B, wb), done) in enumerate(zip(ms, dones)):
                    DV.wait(done, l_cst, T.get(("wv", sg - 3)), T.get("ll_used"))
                    DV.run(cp(V[sg % 3][:, c, :], B[:, 0:256]))
                    free[m] = DV.run(tt(pre[:, c, :], B[:, 256:464], bv[:, B_LP:B_LP + 208], ALU.mult))
                T["V", sg] = T["pre"] = free[m]
            if j == 1:
                DV.wait(T["pre"])
                a = DV.run(tt(pre[:, :, :], pre[:, :, :], bc(bv[:, B_BI:B_BI + 208], 1, 2), ALU.add))
                DV.wait(a)
                a = DV.run(stt(t1[:, :, :], pre[:, :, :], -1.0, pre[:, :, :], ALU.mult, ALU.max))
                AC.wait(a)
                a = AC.run(act(t2[:, :, :], t1[:, :, :], ACT.Exp, scale=-1.0))
                T["u"] = a
                AC.wait(a)
                a = AC.run(act(t3[:, :, :], t2[:, :, :], ACT.Ln, bias=1.0))
                AC.wait(a)
                T["lw"] = AC.run(act(t4[:, :, :], t3[:, :, :], ACT.Exp, scale=-1.0))
            if j == 2:
                DV.wait(T["u"])
                a = DV.run(ts(t1[:, :, :], t2[:, :, :], 1.0, None, ALU.add))
                DV.wait(a)
                b1 = DV.run(stt(t5[:, :, :], t1[:, :, :], -1.0, t2[:, :, :], ALU.add, ALU.subtract))
                DV.wait(b1, T["lw"])
                a = DV.run(tt(t4[:, :, :], t4[:, :, :], t5[:, :, :], ALU.mult))
                DV.wait(a)
                a = DV.run(tt(t3[:, :, :], t3[:, :, :], t4[:, :, :], ALU.subtract))
                DV.wait(a)
                T["sp"] = DV.run(stt(t3[:, :, :], pre[:, :, :], 0.0, t3[:, :, :], ALU.max, ALU.add))
                sp4 = t3[:, :, :].rearrange("p c (h l) -> p c h l", l=NL)
                DV.wait(T["sp"], T["eA"])
                T["gg"] = DV.run(stt(gg[:, :, :], sp4[:, :, :, LV], -1.0, bc(eA[:, :], 1, 2), ALU.mult, ALU.mult))
                b1 = DV.run(ts(t1[:, :, :], t3[:, :, :], TINY, None, ALU.max))
                T["xm"] = DV.run(ts(t4[:, :, :], pre[:, :, :], LN2_64, 0.0, ALU.add, ALU.min))
                AC.wait(b1)
                T["ln"] = AC.run(act(t2[:, :, :], t1[:, :, :], ACT.Ln))
            if j == 3:
                m, B, wb = misc()
                g2 = gg[:, :, :].rearrange("p c h -> p (c h)")
                done, = yield [([T["gg"], l_cst, wb], [mm(B[:, 0:32], cs[:, C_TRI:C_TRI + 128], g2),
                                                      mm(B[:, 32:64], cs[:, C_ONE:C_ONE + 128], g2)])]
                DV.wait(done, T.get("cgt_used"))
                free[m] = T["cgt"] = DV.run(cp(cgt[:, :, :].rearrange("p a n -> p (a n)"), B[:, 0:64]))
            if j == 4:
                cg = cgt[:, 0, :].rearrange("p (c h) -> p c h", c=2)
                tot = cgt[:, 1, :].rearrange("p (c h) -> p c h", c=2)
                DV.wait(T["cgt"], T.get("ll_used"), T["ln"], T.get(("exp", sg - 2)), T.get("dcol_used"))
                T["ncg", sg] = DV.run(ts(ncg[b][:, :, :], cg, -1.0, None, ALU.mult))
                a1 = DV.run(tt(dcol[:, :, :], tot, cg, ALU.subtract))
                a = DV.run(tt(t2[:, :, :], t2[:, :, :], t4[:, :, :], ALU.add))
                DV.wait(a)
                cgc = cgt[:, 0, :]
                T["ll"] = DV.run(tt(ll[:, :, :].rearrange("p c (h l) -> p (c h) l", l=NL),
                                    t2[:, :, :].rearrange("p c (h l) -> p (c h) l", l=NL),
                                    bc(cgc, 2, NL), ALU.add))
                AC.wait(a1, T["cgt"], T["ll"], T.get(("state", sg - 2)), T.get(("inter", sg - 2)), T.get("dv_used"))
                a = AC.run(act(dv[:, :, :], dcol[:, :, :], ACT.Exp))
                T["dcol_used"] = T["dv"] = a
                AC.run(act(dec[b][0:64, :, :], cgt[0:64, 1, :].rearrange("p (c q e) -> p c q e", c=2, e=2)[:, :, :, 0],
                           ACT.Exp))
                T["dec", sg] = T["cgt_used"] = AC.run(
                    act(dec[b][64:128, :, :], cgt[64:128, 1, :].rearrange("p (c q e) -> p c q e", c=2, e=2)[:, :, :, 1],
                        ACT.Exp))
                T["coef", sg] = AC.run(
                    act(coef[b][:, :, :, :].rearrange("p c h b -> p (c h) b"),
                        ll[:, :, :].rearrange("p c (h l) -> p (c h) l", l=NL)[:, :, 8:12], ACT.Exp))
            if j in (5, 7):
                c = (j - 5) // 2
                l3 = ll[:, c, :].rearrange("p (h l) -> p h l", l=NL)
                GP.wait(T["ll"], l_cst, T.get("red"))
                a = GP.run(tt(lfp[:, :].rearrange("p (h s l) -> p h s l", h=H, s=16), bc(l3[:, :, 0:5], 2, 16),
                              bc(cs[:, C_MF:C_MF + 80].rearrange("p (s l) -> p s l", l=5), 1, H), ALU.mult))
                b1 = GP.run(tt(lcp[:, :].rearrange("p (h s l) -> p h s l", h=H, s=8), bc(l3[:, :, 5:8], 2, 8),
                               bc(cs[:, C_MC:C_MC + 24].rearrange("p (s l) -> p s l", l=3), 1, H), ALU.mult))
                T["prod"] = (a, b1)
                if c == 1:
                    T["ll_used"] = b1
                T["todo"] = (2 * sg + c, a, b1)
            if j == 5:
                DV.wait(T["dv"], T["V", sg], T.get(("state", sg - 2)))
                T["Vw", sg] = T["dv_used"] = DV.run(
                    tt(Vw[b][:, :, :].rearrange("p c (h d) -> p (c h) d", h=H),
                       V[sg % 3][:, :, :].rearrange("p c (h d) -> p (c h) d", h=H),
                       bc(dv[:, :, :].rearrange("p c h -> p (c h)"), 2, 16), ALU.mult))

        def reduce_levels():
            ci, a, b1 = T.pop("todo")
            n = ci % 4
            DV.wait(a, b1, T.get(("xbuilt", ci - 4)))
            a = DV.run(lambda e: e.tensor_reduce(Lf[n][:, :, :], lfp[:, :].rearrange("p (h s l) -> p h s l", h=H, s=16),
                                                 AX.X, ALU.add))
            b1 = DV.run(lambda e: e.tensor_reduce(Lc[n][:, :, :], lcp[:, :].rearrange("p (h s l) -> p h s l", h=H, s=8),
                                                  AX.X, ALU.add))
            T["red"] = b1
            DV.wait(a, b1)
            DV.run(tt(Lf[n][:, :, :], Lf[n][:, :, :], bc(cs[:, C_NF:C_NF + 16], 1, H), ALU.add))
            T["L", ci] = DV.run(tt(Lc[n][:, :, :], Lc[n][:, :, :], bc(cs[:, C_NC:C_NC + 8], 1, H), ALU.add))

        def exponents(G):
            ci, g = G // 4, G % 4
            c, h0, i = ci % 2, heads_of(G % 4)[0], G % 3
            x4 = X[i][:, :].rearrange("p (h b s) -> p h b s", h=4, b=8)
            GP.wait(T["L", ci], T.get(("xt", G - 3)))
            a = GP.run(tt(x4, bc(Lf[ci % 4][:, h0:h0 + 7:2, :], 2, 8),
                          cs[:, C_OWN:C_OWN + 8].unsqueeze(1).unsqueeze(3).broadcast_to([P, 4, 8, 16]), ALU.mult))
            GP.wait(a)
            T["x", G] = GP.run(tt(x4, x4, bc(Lc[ci % 4][:, h0:h0 + 7:2, :], 3, 16), ALU.add))
            if g == 3:
                T["xbuilt", ci] = T["x", G]

        def qk_ready(sg):
            return [T["QT", sg, 6], T["KT", sg, 7]]

        def scores(G):
            ci, g, i = G // 4, G % 4, G % 2
            sg, c, b = ci // 2, ci % 2, (ci // 2) % 2
            hs = heads_of(g)
            r = 64 * (hs[0] % 2)
            PE.wait(T.get(("w", G - 2)), *qk_ready(sg))
            T["p", G] = PE.run(*[
                mm(PB[i][:, 128 * n:128 * n + 128], KT[b][r:r + 64, h // 2, 128 * c:128 * c + 128],
                   QT[b][r:r + 64, h // 2, 128 * c:128 * c + 128]) for n, h in enumerate(hs)])
            PE.wait(T["x", G], T.get(("e", G - 2)))
            T["xt", G] = PE.run(*[tr(XB[i][:, 128 * n:128 * n + 128], X[G % 3][:, 128 * n:128 * n + 128])
                                  for n in range(4)])
            AC.wait(T["xt", G], T["ncg", sg], T.get(("w", G - 2)))
            T["e", G] = AC.run(*[act(E[i][:, 128 * n:128 * n + 128], XB[i][:, 128 * n:128 * n + 128], ACT.Exp,
                                     bias=ncg[b][:, c, h:h + 1]) for n, h in enumerate(hs)])
            if c == 1 and g == 3:
                T["exp", sg] = T["e", G]

        def weights(G):
            i = G % 2
            DV.wait(T["p", G], T["e", G], T.get(("y", G - 2)))
            T["w", G] = DV.run(tt(W[i][:, :], PB[i][:, :], E[i][:, :], ALU.mult))

        def weigh(G):
            ci, g, i = G // 4, G % 4, G % 2
            sg, c, b = ci // 2, ci % 2, (ci // 2) % 2
            waits = [T["w", G], T["V", sg]]
            if g == 0:
                waits.append(T.get(("yf", ci - 1)))
            T["y", G], = yield [(waits, [mm(YB[:, 16 * h:16 * h + 16], W[i][:, 128 * n:128 * n + 128],
                                            V[sg % 3][:, c, 16 * h:16 * h + 16]) for n, h in enumerate(heads_of(g))])]
            if c == 1 and g == 3:
                T["wv", sg] = T["y", G]

        def keys(ci):
            sg, c, b = ci // 2, ci % 2, (ci // 2) % 2
            ms = [misc() for n in range(2)]
            dones = yield [(qk_ready(sg) + [w], [tr(B[:, 128 * q:128 * q + 128], KT[b][:, 4 * n + q, 128 * c:128 * c + 128])
                                                for q in range(4)]) for n, (m, B, w) in enumerate(ms)]
            for n, ((m, B, w), done) in enumerate(zip(ms, dones)):
                AC.wait(done, T.get("kt_used"))
                free[m] = AC.run(act(Kt[:, 512 * n:512 * n + 512], B[:, :], ACT.Copy))
            T["kt"] = free[m]

        def inter(ci):
            cc = ci % CB
            sg, c, b = ci // 2, ci % 2, (ci // 2) % 2
            nb = cc.bit_length()
            if nb == 0:
                return
            zs, ms, jobs = [], [], []
            for e2 in range(2):
                m, B, wb = misc()
                ms.append(m)
                jobs.append(([T["Sd"], wb], [
                    mm(B[:, 128 * p:128 * p + 32 * nb], QT[b][:, 4 * e2 + p, 128 * c:128 * c + 128],
                       Sd[:, 4 * e2 + p, :, 0:16 * nb]) for p in range(4)]))
            dones = yield jobs
            for e2, (m, done) in enumerate(zip(ms, dones)):
                B = MB[m]
                DV.wait(done, T["coef", sg], T.get("zr_done"))
                n = 8 * nb * 16
                for e in range(2):
                    zv = zt[:, n * e2:n * e2 + n].rearrange("p (q e n) -> p q e n", q=4, e=2)[:, :, e, :]
                    zsrc = B[:, :].rearrange("p (q n) -> p q n", q=4)[:, :, 16 * nb * e:16 * nb * e + 16 * nb]
                    free[m] = DV.run(tt(zv.rearrange("p q (b d) -> p q b d", d=16),
                                        zsrc.rearrange("p q (b d) -> p q b d", d=16),
                                        bc(coef[b][:, c, 8 * e2 + e:8 * e2 + 8:2, 0:nb], 3, 16), ALU.mult))
                zs.append(free[m])
            T["S_read"] = done
            if c == 1:
                T["inter", sg] = free[m]
            DV.wait(*zs, T.get(("yf", ci - 2)))
            T["zr", ci] = T["zr_done"] = DV.run(lambda e: e.tensor_reduce(
                zr[ci % 2][:, :].rearrange("p (h d) -> p h d", d=16),
                zt[:, 0:16 * nb * 16].rearrange("p (h b d) -> p h d b", h=H, d=16), AX.X, ALU.add))

        def state(ci):
            cc = ci % CB
            sg, c, b = ci // 2, ci % 2, (ci // 2) % 2
            if cc < CB - 1:
                nb, z = cc.bit_length(), ((cc + 1) & -(cc + 1)).bit_length() - 1
                m, B, wb = misc()
                done, = yield [([T["kt"], T["Vw", sg], wb],
                                [mm(B[:, 32 * p:32 * p + 32], Kt[:, 128 * p:128 * p + 128],
                                    Vw[b][:, c, 32 * p:32 * p + 32]) for p in range(8)])]
                T["kt_used"] = done
                DV.wait(T["dec", sg], T.get("Sd"), T.get("S"))
                a = None
                if nb:
                    s3 = S[:, :, 0:nb, :].rearrange("p q b d -> p q (b d)")
                    a = DV.run(tt(s3, s3, bc(dec[b][:, c, :], 2, 16 * nb), ALU.mult))
                DV.wait(done, a)
                for e2 in range(2):
                    r = slice(64 * e2, 64 * e2 + 64)
                    src = B[r, 0:256].rearrange("p (q n) -> p q n", q=8)[:, :, 16 * e2:16 * e2 + 16]
                    if z == 0:
                        a = DV.run(cp(S[r, :, 0, :], src))
                    else:
                        a = DV.run(tt(S[r, :, z, :], src, S[r, :, 0, :], ALU.add))
                free[m] = a
                for l in range(1, z):
                    DV.wait(a)
                    a = DV.run(tt(S[:, :, z, :], S[:, :, z, :], S[:, :, l, :], ALU.add))
                if z:
                    DV.wait(a)
                    a = DV.run(lambda e: e.memset(S[:, :, 0:z, :], 0.0))
                T["S"] = a
                AC.wait(a, T.get("S_read"), T["Sd0"])
                nx = (cc + 1).bit_length()
                for e2 in range(2):
                    r = slice(64 * e2, 64 * e2 + 64)
                    T["Sd"] = AC.run(act(Sd[r, :, e2, 0:16 * nx], S[r, :, 0:nx, :].rearrange("p q b d -> p q (b d)"),
                                         ACT.Copy))
                if c == 1:
                    T["state", sg] = a
            elif c == 1:
                T["state", sg] = T["S"]

        def gather(ci):
            cc = ci % CB
            DV.wait(T["y", 4 * ci + 3], T.get("yt_done"))
            if cc:
                DV.wait(T["zr", ci])
                T["yf", ci] = DV.run(tt(yf[:, :], YB[:, 0:256], zr[ci % 2][:, :], ALU.add))
            else:
                T["yf", ci] = DV.run(cp(yf[:, :], YB[:, 0:256]))

        def turn_y(ci):
            m, B, wb = misc()
            PE.wait(wb)
            PE.wait(T["yf", ci])
            done = PE.run(*[tr(B[:, 128 * k:128 * k + 128], yf[:, 128 * k:128 * k + 128]) for k in range(2)])
            T["yt_done"] = done
            AC.wait(done, T.get("op_done"))
            free[m] = T["yt"] = AC.run(act(yt[:, :], B[:, 0:256], ACT.Copy))

        def norm(o, i, st, mv, lr, rs, key, used):
            a = DV.run(lambda e: e.bn_stats(st[:, :], i))
            DV.wait(a, used)
            a = DV.run(lambda e: e.bn_aggr(mv[:, :], st[:, :]))
            GP.wait(a, l_cst)
            a = GP.run(tt(lr[:, :], mv[:, 1:2], cs[:, C_EPS:C_EPS + 1], ALU.add))
            GP.wait(a)
            T[key] = GP.run(tt(rs[:, :], lr[:, :], cs[:, C_HALF:C_HALF + 1], ALU.pow))

        def out_proj(ci):
            m, B, wb = misc()
            PE.wait(wb)
            PE.wait(T["yt"], l_wo)
            done = PE.run(*[mm(B[:, 0:256], yt[:, 128 * k:128 * k + 128], wo[:, k, :], start=(k == 0), stop=(k == 1))
                            for k in range(2)])
            T["op_done"] = done
            DV.wait(done, l_x[ci // 2])
            free[m] = DV.run(tt(oo[:, :], B[:, 0:256], xs[:, ci, :], ALU.add))
            DV.wait(free[m])
            norm(None, oo[:, :], st1, mv1, lr1, rs1, "rs1", None)

        def normalise(ci):
            DV.wait(T["rs1"], T.get("nn_used"))
            a = DV.run(ts(nn[:, :], oo[:, :], mv1[:, 0:1], rs1[:, 0:1], ALU.subtract, ALU.mult))
            GP.wait(a, l_x[ci // 2], T.get("x1_used"))
            a = GP.run(tt(nn[:, :], nn[:, :], bv[:, B_G:B_G + 256], ALU.mult))
            GP.wait(a)
            a = GP.run(tt(nn[:, :], nn[:, :], bv[:, B_B:B_B + 256], ALU.add))
            GP.wait(a)
            T["x1"] = T["nn_used"] = GP.run(tt(x1[:, :], nn[:, :], xs[:, ci, :], ALU.add))

        def outer_stats(ci):
            DV.wait(T["x1"])
            norm(None, x1[:, :], st2, mv2, lr2, rs2, "rs2", None)

        def outer_norm(ci):
            DV.wait(T["rs2"])
            T["x2", ci] = T["x1_used"] = DV.run(
                ts(xs[:, ci, :], x1[:, :], mv2[:, 0:1], rs2[:, 0:1], ALU.subtract, ALU.mult))

        def turn_x(ci):
            m, B, wb = misc()
            PE.wait(wb)
            PE.wait(T["x2", ci])
            done = PE.run(*[tr(B[:, 128 * k:128 * k + 128], xs[:, ci, 128 * k:128 * k + 128]) for k in range(2)])
            AC.wait(done)
            free[m] = T["x2t", ci] = AC.run(act(xts[:, :, 128 * ci:128 * ci + 128],
                                                B[:, 0:256].rearrange("p (k t) -> p k t", k=2), ACT.Copy))

        def together(parts):
            jobs = [next(p, []) for p in parts]
            tokens = PE.weave(*[q for js in jobs for q in js])
            for p, js in zip(parts, jobs):
                mine, tokens = tokens[:len(js)], tokens[len(js):]
                if js:
                    try:
                        p.send(mine)
                    except StopIteration:
                        pass

        tail = {5: gather, 7: turn_y, 9: out_proj, 10: normalise, 11: outer_stats, 12: outer_norm, 14: turn_x}
        NG = 4 * NC
        for s in range(-13, NG + 15):
            sg, j = (s + 8) // 8, (s + 8) % 8
            if 0 <= s - 1 < NG:
                weights(s - 1)
            if "todo" in T:
                reduce_levels()
            if 0 <= s < NG:
                scores(s)
            parts = []
            if 0 <= sg < NSG:
                parts.append(project(sg, j))
            if 0 <= s < NG and s % 4 < 3:
                parts.append([keys, inter, state][s % 4](s // 4))
            if 0 <= s - 2 < NG:
                parts.append(weigh(s - 2))
            if (s + 13) // 8 < NSG:
                parts.append(tokens((s + 13) // 8, (s + 13) % 8))
            if 0 <= s + 2 < NG:
                exponents(s + 2)
            together(parts)
            for d, f in tail.items():
                if s - d >= 0 and (s - d) % 4 == 0 and (s - d) // 4 < NC:
                    f((s - d) // 4)
            if 0 <= s < NG and s % 8 == 7:
                T["heads", s // 8] = T["p", s]

        w = wq[:, :, :].rearrange("p k (w n) -> p k w n", w=8)
        s_wf = sem("l_wf")
        SY.wait(T["heads", NSG - 1])
        SY.todo.append(lambda e: e.dma_start(w, wffn.rearrange("(k p) w n -> p k w n", p=P)).then_inc(s_wf, 16))
        l_wf = (s_wf, 16)
        WF, WI, WC, UF, UI, UC, WO, UO = range(8)
        b0 = sb("b0", [P, 2, 3])
        gb = [[QT[i][:, 2 * n:2 * n + 2, :].rearrange("p m t -> p (m t)") for n in range(3)] for i in range(2)]
        cells = [KT[i][:, :, :].rearrange("p (c k u) t -> p c k (u t)", c=2, k=2) for i in range(2)]
        c1 = [cells[0][:, i, :, :] for i in range(2)]
        c2 = [cells[1][:, i, :, :] for i in range(2)]
        cu = [sb(f"cu{i}", [P, 256]) for i in range(2)]
        hh = [sb(f"hh{i}", [P, 512]) for i in range(2)]
        st3 = sb("st3", [P, 4, 6])
        mv3 = sb("mv3", [P, NC, 2])
        rs3 = sb("rs3", [P, NC])
        lr3 = sb("lr3", [P, NC])
        ring = [banks[0:3], banks[3:6]]
        bank_free = [[free["Q"], T["w", 4 * NC - 2], T["w", 4 * NC - 1]],
                     [T["e", 4 * NC - 2], T["e", 4 * NC - 1], T["yf", NC - 1]]]
        c0 = fvs[:, 6:8]
        m, B, wb = misc()
        PE.wait(wb)
        PE.wait(l_wf)
        ins = []
        for mt in range(2):
            for n in range(3):
                for k in range(2):
                    ins.append(mm(B[:, 3 * mt + n:3 * mt + n + 1], w[:, k, UF + n, 128 * mt:128 * mt + 128],
                                  c0[:, k:k + 1], start=(k == 0), stop=(k == 1)))
        done = PE.run(*ins)
        DV.wait(done)
        free[m] = T["b0"] = DV.run(tt(b0[:, :, :].rearrange("p m n -> p (m n)"), B[:, 0:6], fvs[:, 0:6], ALU.add))
        cell = [0]

        def gates(blk, t):
            a0 = 2048 * t + 512 * blk
            for mt in range(2):
                i = cell[0] % 2
                cell[0] += 1
                res = []
                for n in range(3):
                    PE.wait(bank_free[i][n], *[T["x2t", 16 * t + 4 * blk + q] for q in range(4)])
                    ops = [(w[:, k, WF + n, 128 * mt:128 * mt + 128], xts[:, k, a0:a0 + 512]) for k in range(2)]
                    if t:
                        PE.wait(T["c1", blk])
                        ops += [(w[:, k, UF + n, 128 * mt:128 * mt + 128], c1[blk % 2][:, k, :]) for k in range(2)]
                    done = PE.run(*[mm(ring[i][n][:, :], l, r, start=(q == 0), stop=(q == len(ops) - 1))
                                    for q, (l, r) in enumerate(ops)])
                    AC.wait(done, T["b0"], T.get(("cell", i)))
                    bias = fvs[:, 3 * mt + n:3 * mt + n + 1] if t else b0[:, mt, n:n + 1]
                    bank_free[i][n] = AC.run(act(gb[i][n], ring[i][n][:, :], ACT.Tanh if n == 2 else ACT.Sigmoid,
                                                 bias=bias))
                    res.append(bank_free[i][n])
                DV.wait(*res)
                a = DV.run(tt(gb[i][1], gb[i][1], gb[i][2], ALU.mult))
                if t == 0:
                    DV.wait(a, T.get(("gates1", blk - 2)))
                    T["cell", i] = DV.run(stt(c1[blk % 2][:, mt, :], gb[i][0], c0[:, mt:mt + 1], gb[i][1],
                                              ALU.mult, ALU.add))
                else:
                    a1 = DV.run(tt(gb[i][0], gb[i][0], c1[blk % 2][:, mt, :], ALU.mult))
                    DV.wait(a, a1, T.get(("out", blk - 2)))
                    T["cell", i] = DV.run(tt(c2[blk % 2][:, mt, :], gb[i][0], gb[i][1], ALU.add))
            if t == 0:
                T["c1", blk] = T["cell", i]
            else:
                T["gates1", blk] = done
                T["c2", blk] = T["cell", i]

        def outputs(blk):
            for q in range(4):
                tt_ = 4 * blk + q
                i = tt_ % 2
                cT = c2[blk % 2]
                m, B, wb = misc()
                PE.wait(wb)
                PE.wait(T["c2", blk])
                done = PE.run(*[mm(B[:, 0:256], cT[:, k, 128 * q:128 * q + 128], w[:, k, UO, :],
                                   start=(k == 0), stop=(k == 1)) for k in range(2)])
                DV.wait(done, T.get(("cu", i)))
                free[m] = a0 = DV.run(tt(cu[i][:, :], B[:, 0:256], bv[:, B_BO:B_BO + 256], ALU.add))
                m, B, wb = misc()
                PE.wait(wb)
                done = PE.run(*[mm(B[:, 256 * t:256 * t + 256], xts[:, k, 2048 * t + 128 * tt_:2048 * t + 128 * tt_ + 128],
                                   w[:, k, WO, :], start=(k == 0), stop=(k == 1)) for t in range(2) for k in range(2)])
                h3 = hh[i][:, :].rearrange("p (t n) -> p t n", t=2)
                DV.wait(done, a0, T.get(("hh", i)))
                free[m] = T["cu", i] = DV.run(tt(h3, B[:, :].rearrange("p (t n) -> p t n", t=2), bc(cu[i][:, :], 1, 2),
                                                 ALU.add))
                AC.wait(free[m])
                a = AC.run(act(hh[i][:, :], hh[i][:, :], ACT.Tanh))
                GP.wait(a)
                dst = xs[:, tt_:tt_ + 17:16, :]
                T["hh", i] = a = GP.run(tt(dst, dst, h3, ALU.add))
                DV.wait(a)
                s2 = [DV.run(lambda e, t=t, i=i, tt_=tt_: e.bn_stats(st3[:, 2 * i + t, :], xs[:, tt_ + 16 * t, :])) for t in range(2)]
                DV.wait(*s2)
                for t in range(2):
                    a = DV.run(lambda e, t=t, i=i, tt_=tt_: e.bn_aggr(mv3[:, tt_ + 16 * t, :], st3[:, 2 * i + t, :]))
                T["mv3", tt_] = a
            T["out", blk] = done

        gates(0, 0)
        for blk in range(4):
            if blk < 3:
                gates(blk + 1, 0)
            gates(blk, 1)
            if blk:
                outputs(blk - 1)
        outputs(3)
        GP.wait(T["mv3", 15])
        a = GP.run(tt(lr3[:, :], mv3[:, :, 1], cs[:, C_EPS:C_EPS + 1].broadcast_to([P, NC]), ALU.add))
        GP.wait(a)
        a = GP.run(tt(rs3[:, :], lr3[:, :], cs[:, C_HALF:C_HALF + 1].broadcast_to([P, NC]), ALU.pow))
        DV.wait(a)
        ov = out.rearrange("(n p) d -> p n d", p=P)
        s_out = sem("s_out")
        for n in range(NC):
            a = DV.run(ts(xs[:, n, :], xs[:, n, :], mv3[:, n, 0:1], rs3[:, n:n + 1], ALU.subtract, ALU.mult))
            if n % 2:
                SY.wait(a)
                SY.todo.append(lambda e, n=n: e.dma_start(ov[:, n - 1:n + 1, :], xs[:, n - 1:n + 1, :]).then_inc(s_out, 16))
        SY.wait((s_out, 16 * (NC // 2)))

        block = ctx.enter_context(nc.Block())

        @block.sync
        def _(e):
            SY.replay(e)

        @block.tensor
        def _(e):
            PE.replay(e)

        @block.vector
        def _(e):
            DV.replay(e)

        @block.scalar
        def _(e):
            AC.replay(e)

        @block.gpsimd
        def _(e):
            GP.replay(e)


def constants():
    c = np.zeros((P, C_END), np.float32)
    t = np.arange(P)
    c[:, C_TRI:C_TRI + 128] = t[:, None] <= t[None, :]
    c[:, C_ONE:C_ONE + 128] = 1.0
    c[:, C_ID:C_ID + 128] = np.eye(P)

    def level(a, b):
        v = a ^ b
        return int(v).bit_length()

    for p in range(P):
        for b in range(8):
            k = p // 16
            if b < k:
                c[p, C_MC + 3 * b + level(k, b) - 1] = 1.0
            if b > k:
                c[p, C_NC + b] = NEG
            if b == k:
                c[p, C_OWN + b] = 1.0
        for s in range(16):
            if s <= p % 16:
                c[p, C_MF + 5 * s + level(p % 16, s)] = 1.0
            else:
                c[p, C_NF + s] = NEG
    c[:, C_EPS] = EPS
    c[:, C_HALF] = -0.5
    return c


def kernel(**a):
    import concourse.bacc as bacc
    from concourse.bass_utils import run_bass_kernel_spmd

    a = {k: np.asarray(v) for k, v in a.items()}
    f = {k.replace("L0_attn_", "").replace("L0_ffn_", "f_"): v for k, v in a.items()}
    x = np.ascontiguousarray(f["x"].reshape(NT, 256))
    dlt = np.concatenate([f["Wdl"].reshape(H, LV, 256), f["Wdt"].reshape(H, 1, 256)], 1).reshape(H * NL, 256)
    lp = np.concatenate([f["Lp"], np.ones((H, 1), np.float32)], 1).reshape(-1)
    bi = np.concatenate([np.zeros((H, LV), np.float32), f["dt_bias"].reshape(H, 1)], 1).reshape(-1)
    row = np.concatenate([lp, bi, f["A_log"], f["ln_g"], f["ln_b"], f["f_bo"]])
    fv = np.concatenate([np.stack([f["f_bf"], f["f_bi"], f["f_bc"]], 1).reshape(2, P, 3).transpose(1, 0, 2).reshape(P, 6),
                         f["f_in_c"].reshape(2, P).T], 1)
    data = {
        "x": x,
        "xT": x.T,
        "wqk": np.concatenate([f["Wq"], f["Wk"]], 0).T,
        "wtok": np.concatenate([f["Wv"], dlt], 0).T,
        "wout": f["Wout"].T,
        "wffn": np.stack([f["f_" + n].T for n in ("wf", "wi", "wc", "uf", "ui", "uc", "wo", "uo")], 1),
        "cst": constants(),
        "bcv": np.broadcast_to(row, (P, B_END)),
        "fv": fv,
    }
    data = {k: np.ascontiguousarray(v) for k, v in data.items()}
    nc = bacc.Bacc("TRN2", target_bir_lowering=False, num_devices=1)
    aps = [nc.dram_tensor("in_" + k, v.shape, F32, kind="ExternalInput").ap() for k, v in data.items()]
    aps.append(nc.dram_tensor("out_0", (NT, 256), F32, kind="ExternalOutput").ap())
    program(nc, *aps)
    r = run_bass_kernel_spmd(nc, [{"in_" + k: v for k, v in data.items()}], core_ids=[0])
    return r.results[0]["out_0"].reshape(2, 2048, 256)
```

```python
import numpy as np
import concourse.bass as bass
from concourse import mybir
from contextlib import ExitStack

P = 128
F32 = mybir.dt.float32
F32R = mybir.dt.float32r
ALU = mybir.AluOpType
ACT = mybir.ActivationFunctionType
AX = mybir.AxisListType
H = 16
LV = 12
NL = LV + 1
NT = 4096
NC = NT // P
CB = 16
NSG = NC // 2
NEG = -1.0e30
LN2_64 = 64.0 * float(np.log(2.0))
TINY = 2.0 ** -64
EPS = 1e-5

C_TRI, C_ONE, C_ID = 0, 128, 256
C_MC, C_MF, C_NC, C_NF, C_OWN, C_EPS = 384, 408, 488, 496, 512, 520
C_HALF, C_END = 521, 522
B_LP, B_BI, B_AL, B_G, B_B, B_BO = 0, 208, 416, 432, 688, 944
B_END = 1200


def heads_of(g):
    return [8 * (g // 2) + (g % 2) + 2 * i for i in range(4)]


class Engine:

    def __init__(self, name, sem):
        self.name, self.sem, self.count, self.todo, self.seen = name, sem, 0, [], {}

    def wait(self, *tokens):
        for sem, value in [t for t in tokens if t is not None]:
            if self.seen.get(sem.name, 0) < value:
                self.seen[sem.name] = value
                self.todo.append(lambda e, s=sem, v=value: e.wait_ge(s, v))

    def run(self, *instructions):
        for f in instructions[:-1]:
            self.todo.append(f)
        self.count += 1
        self.todo.append(lambda e, f=instructions[-1]: f(e).then_inc(self.sem, 1))
        return (self.sem, self.count)

    def weave(self, *jobs):
        most = max([len(ins) for _, ins in jobs] + [1])
        order = sorted(((n + 0.5) * most / len(ins), k, n) for k, (_, ins) in enumerate(jobs) for n in range(len(ins)))
        tokens = [None] * len(jobs)
        for _, k, n in order:
            waits, ins = jobs[k]
            if n == 0:
                self.wait(*waits)
            if n == len(ins) - 1:
                tokens[k] = self.run(ins[n])
            else:
                self.todo.append(ins[n])
        return tokens

    def replay(self, e):
        for f in self.todo:
            f(e)


def bc(ap, axis, n):
    shape = list(ap.shape)
    shape.insert(axis, n)
    return ap.unsqueeze(axis).broadcast_to(shape)


def program(nc, x, xT, wqk, wtok, wout, wffn, cst, bcv, fv, out):
    ctx = ExitStack()
    with ctx:
        def sb(name, shape, dt=F32):
            return ctx.enter_context(nc.sbuf_tensor(name, shape, dt))

        def sem(name):
            return ctx.enter_context(nc.semaphore(name))

        banks = [ctx.enter_context(nc.psum_tensor(f"bank{i}", [P, 512], F32)) for i in range(8)]
        PB, XB, YB, MB = banks[1:3], banks[3], banks[4:6], banks[6:8]

        xs = sb("xs", [P, NC, 256])
        wH, wL = [sb(n, [P, 2, 2048], F32R) for n in ("wH", "wL")]
        wtH, wtL = [sb(n, [P, 2, 464], F32R) for n in ("wtH", "wtL")]
        xt = [sb(f"xt{i}", [P, 2, 256]) for i in range(3)]
        wo = sb("wo", [P, 2, 256])
        cs = sb("cs", [P, C_END])
        bv = sb("bv", [P, B_END])
        fvs = sb("fvs", [P, 8])
        yf = sb("yf", [P, 256])
        yt = sb("yt", [P, 256])
        oo = sb("oo", [P, 256])
        nn = sb("nn", [P, 256])
        x1 = sb("x1", [P, 256])
        st1 = sb("st1", [P, 6])
        mv1 = sb("mv1", [P, 2])
        lr1 = sb("lr1", [P, 1])
        rs1 = sb("rs1", [P, 1])
        st2 = sb("st2", [P, 6])
        mv2 = sb("mv2", [P, 2])
        lr2 = sb("lr2", [P, 1])
        rs2 = sb("rs2", [P, 1])
        b0 = sb("b0", [P, 2, 3])
        c0H, c0L = [sb(n, [P, 2, 128], F32R) for n in ("c0H", "c0L")]
        mv3 = sb("mv3", [P, NC, 2])
        rs3 = sb("rs3", [P, NC])
        lr3 = sb("lr3", [P, NC])

        first = ExitStack()

        def sb(name, shape, dt=F32):
            return first.enter_context(nc.sbuf_tensor(name, shape, dt))

        xH, xL = [[sb(f"{n}{i}", [P, 2, 256], F32R) for i in range(2)] for n in ("xH", "xL")]
        QT = [sb(f"QT{i}", [P, 8, 256]) for i in range(2)]
        KT = [sb(f"KT{i}", [P, 8, 256]) for i in range(2)]
        Kt = sb("Kt", [P, 1024])
        V = [sb(f"V{i}", [P, 2, 256]) for i in range(3)]
        Vw = [sb(f"Vw{i}", [P, 2, 256]) for i in range(2)]
        pre = sb("pre", [P, 2, 208])
        t1 = sb("t1", [P, 2, 208])
        t2 = sb("t2", [P, 2, 208])
        t3 = sb("t3", [P, 2, 208])
        t4 = sb("t4", [P, 2, 208])
        t5 = sb("t5", [P, 2, 208])
        ll = sb("ll", [P, 2, 208])
        eA = sb("eA", [P, H])
        gg = sb("gg", [P, 2, H])
        cgt = sb("cgt", [P, 2, 2 * H])
        ncg = [sb(f"ncg{i}", [P, 2, H]) for i in range(2)]
        dcol = sb("dcol", [P, 2, H])
        dv = sb("dv", [P, 2, H])
        dec = [sb(f"dec{i}", [P, 2, 8]) for i in range(2)]
        coef = [sb(f"coef{i}", [P, 2, H, 4]) for i in range(2)]
        lfp = sb("lfp", [P, 1280])
        lcp = sb("lcp", [P, 384])
        Lf = [sb(f"Lf{i}", [P, H, 16]) for i in range(4)]
        Lc = [sb(f"Lc{i}", [P, H, 8]) for i in range(4)]
        X = [sb(f"X{i}", [P, 512]) for i in range(3)]
        E = [sb(f"E{i}", [P, 512]) for i in range(2)]
        W = [sb(f"W{i}", [P, 512]) for i in range(2)]
        S = sb("S", [P, 8, 4, 16])
        Sd = sb("Sd", [P, 8, 2, 64])
        zt = sb("zt", [P, 1024])
        zr = [sb(f"zr{i}", [P, 256]) for i in range(2)]
        first.close()

        def sb(name, shape, dt=F32):
            return ctx.enter_context(nc.sbuf_tensor(name, shape, dt))

        yH, yL = [[[sb(f"{n}{t}{i}", [P, 2, 512], F32R) for i in range(2)] for t in range(2)] for n in ("yH", "yL")]
        gb = [[sb(f"g{i}{n}", [P, 512]) for n in range(3)] for i in range(2)]
        c1 = [sb(f"c1{i}", [P, 2, 512]) for i in range(2)]
        c1H, c1L, c2H, c2L = [[sb(f"{n}{i}", [P, 2, 512], F32R) for i in range(2)] for n in ("c1H", "c1L", "c2H", "c2L")]
        cu = [sb(f"cu{i}", [P, 256]) for i in range(2)]
        hh = [sb(f"hh{i}", [P, 512]) for i in range(2)]
        st3 = sb("st3", [P, 4, 6])

        ident = cs[:, C_ID:C_ID + 128]

        PE = Engine("tensor", sem("s_pe"))
        DV = Engine("vector", sem("s_dve"))
        AC = Engine("scalar", sem("s_act"))
        GP = Engine("gpsimd", sem("s_pool"))
        SY = Engine("sync", sem("s_sync"))

        def load(name, *pairs):
            s = sem(name)
            for o, i in pairs:
                SY.todo.append(lambda e, o=o, i=i: e.dma_start(o, i).then_inc(s, 16))
            return (s, 16 * len(pairs))

        def kt(ap):
            return ap.rearrange("(k p) n -> p k n", p=P)

        xv = x.rearrange("(n p) d -> p n d", p=P)
        l_x, l_xt = [], []

        def load_xt(sg):
            SY.wait(T.get(("split", sg - 3)))
            l_xt.append(load(f"l_xt{sg}", (xt[sg % 3][:, :, :], kt(xT)[:, :, 256 * sg:256 * sg + 256])))

        wt0, w0 = QT[0][:, :, :].rearrange("p m t -> p (m t)"), [QT[1], KT[1]]
        T = {}
        l_wt = load("l_wt", (wt0[:, 0:928].rearrange("p (k n) -> p k n", k=2), kt(wtok)))
        load_xt(0)
        l_cst = load("l_cst", (cs[:, :], cst), (bv[:, :], bcv), (fvs[:, :], fv))
        w0v = [t[:, :, :].rearrange("p m t -> p (m t)") for t in w0]
        l_wq = [load(f"l_wq{i}", *[(w0v[k][:, 512 * i:512 * i + 512], kt(wqk)[:, k, 512 * i:512 * i + 512])
                                   for k in range(2)]) for i in (0, 2, 1, 3)]
        l_wq = [l_wq[i] for i in (0, 2, 1, 3)]
        load_xt(1)
        for sg in range(NSG):
            l_x.append(load(f"l_x{sg}", (xs[:, 2 * sg:2 * sg + 2, :], xv[:, 2 * sg:2 * sg + 2, :])))
            if sg == 0:
                l_wo = load("l_wo", (wo[:, :, :], kt(wout)))
        load_xt(2)
        free = {"Q0": None, "Q1": None, "Q2": None, "Q3": None, "Y0": None, "Y1": None, 0: None, 1: None}
        turn = [0]

        def misc():
            m = turn[0] % 2
            turn[0] += 1
            return m, MB[m], free[m]

        def mm(o, a, b, start=True, stop=True):
            return lambda e: e.matmul(o, a, b, start=start, stop=stop)

        def tr(o, i):
            return lambda e: e.transpose(o, i, ident)

        def act(o, i, f, **kw):
            return lambda e: e.activation(o, i, f, **kw)

        def tt(o, a, b, op):
            return lambda e: e.tensor_tensor(o, a, b, op)

        def ts(o, a, s1, s2, op0, op1=None):
            if op1 is None:
                return lambda e: e.tensor_scalar(o, a, s1, None, op0)
            return lambda e: e.tensor_scalar(o, a, s1, s2, op0, op1)

        def stt(o, a, s, b, op0, op1):
            return lambda e: e.scalar_tensor_tensor(out=o, in0=a, scalar=s, in1=b, op0=op0, op1=op1)

        def cp(o, i):
            return lambda e: e.tensor_copy(o, i)

        T["Sd0"] = GP.run(lambda e: e.memset(Sd[:, :, :, :], 0.0))
        AC.todo.append(lambda e: e.preload_act_table_set("natural_log_exp_and_others"))

        def split(hi, lo, src, waits, low=GP):
            AC.wait(*waits)
            a = AC.run(act(hi, src, ACT.Copy))
            low.wait(a, *waits)
            return low.run(tt(lo, src, hi, ALU.subtract))

        def mm3(o, aH, aL, bH, bL, start=True, stop=True):
            return [mm(o, aH, bH, start, False), mm(o, aH, bL, False, False), mm(o, aL, bH, False, stop)]

        def split_x(sg):
            i = sg % 2
            T["split", sg] = split(xH[i][:, :, :], xL[i][:, :, :], xt[sg % 3][:, :, :],
                                   [l_xt[sg], T.get(("projected", sg - 2))], DV)
            if sg + 3 < NSG:
                load_xt(sg + 3)

        def split_wt():
            v = wt0[:, 0:928].rearrange("p (k n) -> p k n", k=2)
            T["wt"] = split(wtH[:, :, :], wtL[:, :, :], v, [l_wt], DV)

        def split_wq(i, low):
            c = slice(512 * i, 512 * i + 512)
            for k in range(2):
                T["wq", i] = split(wH[:, k, c], wL[:, k, c], w0v[k][:, c], [l_wq[i]], low)

        def project(sg, j):
            n = j % 4 if sg == 0 else 0
            b, Q, qb = sg % 2, banks[n], f"Q{n}"
            q = j % 2 == 0
            m0 = j if q else 8 + j - 1
            waits = [T["split", sg], T["wq", m0 // 4], free[qb]]
            ins = []
            for i in range(2):
                c = slice(128 * (m0 + i), 128 * (m0 + i) + 128)
                for k in range(2):
                    ins += mm3(Q[:, 256 * i:256 * i + 256], wH[:, k, c], wL[:, k, c], xH[b][:, k, :], xL[b][:, k, :],
                               k == 0, k == 1)
            done, = yield [(waits, ins)]
            if j == 7:
                T["projected", sg] = done
            src = Q[:, :].rearrange("p (m t) -> p m t", m=2)
            if q:
                AC.wait(done, T.get(("heads", sg - 2)), T["wq", 3] if sg else T["wt"])
                free[qb] = AC.run(act(QT[b][:, m0:m0 + 2, :], src, ACT.Copy, scale=0.125))
                T["QT", sg, j] = free[qb]
            else:
                AC.wait(done, T.get(("heads", sg - 2)), T["wq", 3] if sg else T["wt"])
                free[qb] = AC.run(act(KT[b][:, m0 - 8:m0 - 6, :], src, ACT.Copy))
                T["KT", sg, j] = free[qb]

        def tokens(sg, j):
            b = sg % 2
            if j not in (0, 3):
                yield []
            if j == 0:
                ms = [misc() for c in range(2)]
                dones = yield [([T["split", sg], T["wt"], wb], [
                    f for k in range(2) for f in mm3(
                        B[:, 0:464], xH[b][:, k, 128 * c:128 * c + 128], xL[b][:, k, 128 * c:128 * c + 128],
                        wtH[:, k, :], wtL[:, k, :], k == 0, k == 1)]) for c, (m, B, wb) in enumerate(ms)]
                for c, ((m, B, wb), done) in enumerate(zip(ms, dones)):
                    DV.wait(done, l_cst)
                    a = DV.run(tt(pre[:, c, :], B[:, 256:464], bv[:, B_LP:B_LP + 208], ALU.mult))
                    AC.wait(done, T.get(("wv", sg - 3)), a)
                    free[m] = AC.run(act(V[sg % 3][:, c, :], B[:, 0:256], ACT.Copy))
                T["V", sg], T["pre"] = free[m], a
            if j == 1:
                DV.wait(T["pre"])
                a = DV.run(tt(pre[:, :, :], pre[:, :, :], bc(bv[:, B_BI:B_BI + 208], 1, 2), ALU.add))
                DV.wait(a)
                a = DV.run(stt(t1[:, :, :], pre[:, :, :], -1.0, pre[:, :, :], ALU.mult, ALU.max))
                AC.wait(a)
                a = AC.run(act(t2[:, :, :], t1[:, :, :], ACT.Exp, scale=-1.0))
                T["u"] = a
                AC.wait(a)
                a = AC.run(act(t3[:, :, :], t2[:, :, :], ACT.Ln, bias=1.0))
                AC.wait(a)
                T["lw"] = AC.run(act(t4[:, :, :], t3[:, :, :], ACT.Exp, scale=-1.0))
            if j == 2:
                DV.wait(T["u"])
                a = DV.run(ts(t1[:, :, :], t2[:, :, :], 1.0, None, ALU.add))
                DV.wait(a)
                b1 = DV.run(stt(t5[:, :, :], t1[:, :, :], -1.0, t2[:, :, :], ALU.add, ALU.subtract))
                DV.wait(b1, T["lw"])
                a = DV.run(tt(t4[:, :, :], t4[:, :, :], t5[:, :, :], ALU.mult))
                DV.wait(a)
                a = DV.run(tt(t3[:, :, :], t3[:, :, :], t4[:, :, :], ALU.subtract))
                T["t3"] = a
            if j == 8:
                DV.wait(T["t3"])
                T["sp"] = DV.run(stt(t3[:, :, :], pre[:, :, :], 0.0, t3[:, :, :], ALU.max, ALU.add))
                sp4 = t3[:, :, :].rearrange("p c (h l) -> p c h l", l=NL)
                DV.wait(T["sp"], T["eA"])
                T["gg"] = DV.run(stt(gg[:, :, :], sp4[:, :, :, LV], -1.0, bc(eA[:, :], 1, 2), ALU.mult, ALU.mult))
                b1 = DV.run(ts(t1[:, :, :], t3[:, :, :], TINY, None, ALU.max))
                T["xm"] = DV.run(ts(t4[:, :, :], pre[:, :, :], LN2_64, 0.0, ALU.add, ALU.min))
                AC.wait(b1)
                T["ln"] = AC.run(act(t2[:, :, :], t1[:, :, :], ACT.Ln))
            if j == 3:
                m, B, wb = misc()
                g2 = gg[:, :, :].rearrange("p c h -> p (c h)")
                done, = yield [([T["gg"], l_cst, wb], [mm(B[:, 0:32], cs[:, C_TRI:C_TRI + 128], g2),
                                                      mm(B[:, 32:64], cs[:, C_ONE:C_ONE + 128], g2)])]
                DV.wait(done, T.get("cgt_used"))
                free[m] = T["cgt"] = DV.run(cp(cgt[:, :, :].rearrange("p a n -> p (a n)"), B[:, 0:64]))
            if j == 4:
                cg = cgt[:, 0, :].rearrange("p (c h) -> p c h", c=2)
                tot = cgt[:, 1, :].rearrange("p (c h) -> p c h", c=2)
                DV.wait(T["cgt"], T.get("ll_used"), T["ln"], T.get(("exp", sg - 2)), T.get("dcol_used"))
                T["ncg", sg] = DV.run(ts(ncg[b][:, :, :], cg, -1.0, None, ALU.mult))
                a1 = DV.run(tt(dcol[:, :, :], tot, cg, ALU.subtract))
                a = DV.run(tt(t2[:, :, :], t2[:, :, :], t4[:, :, :], ALU.add))
                DV.wait(a)
                cgc = cgt[:, 0, :]
                T["ll"] = DV.run(tt(ll[:, :, :].rearrange("p c (h l) -> p (c h) l", l=NL),
                                    t2[:, :, :].rearrange("p c (h l) -> p (c h) l", l=NL),
                                    bc(cgc, 2, NL), ALU.add))
                AC.wait(a1, T["cgt"], T["ll"], T.get(("state", sg - 2)), T.get(("inter", sg - 2)), T.get("dv_used"))
                a = AC.run(act(dv[:, :, :], dcol[:, :, :], ACT.Exp))
                T["dcol_used"] = T["dv"] = a
                AC.run(act(dec[b][0:64, :, :], cgt[0:64, 1, :].rearrange("p (c q e) -> p c q e", c=2, e=2)[:, :, :, 0],
                           ACT.Exp))
                T["dec", sg] = T["cgt_used"] = AC.run(
                    act(dec[b][64:128, :, :], cgt[64:128, 1, :].rearrange("p (c q e) -> p c q e", c=2, e=2)[:, :, :, 1],
                        ACT.Exp))
                T["coef", sg] = AC.run(
                    act(coef[b][:, :, :, :].rearrange("p c h b -> p (c h) b"),
                        ll[:, :, :].rearrange("p c (h l) -> p (c h) l", l=NL)[:, :, 8:12], ACT.Exp))
            if j in (5, 7):
                c = (j - 5) // 2
                l3 = ll[:, c, :].rearrange("p (h l) -> p h l", l=NL)
                GP.wait(T["ll"], l_cst, T.get("red"))
                a = GP.run(tt(lfp[:, :].rearrange("p (h s l) -> p h s l", h=H, s=16), bc(l3[:, :, 0:5], 2, 16),
                              bc(cs[:, C_MF:C_MF + 80].rearrange("p (s l) -> p s l", l=5), 1, H), ALU.mult))
                b1 = GP.run(tt(lcp[:, :].rearrange("p (h s l) -> p h s l", h=H, s=8), bc(l3[:, :, 5:8], 2, 8),
                               bc(cs[:, C_MC:C_MC + 24].rearrange("p (s l) -> p s l", l=3), 1, H), ALU.mult))
                T["prod"] = (a, b1)
                if c == 1:
                    T["ll_used"] = b1
                T["todo"] = (2 * sg + c, a, b1)
            if j == 5:
                DV.wait(T["dv"], T["V", sg], T.get(("state", sg - 2)))
                T["Vw", sg] = T["dv_used"] = DV.run(
                    tt(Vw[b][:, :, :].rearrange("p c (h d) -> p (c h) d", h=H),
                       V[sg % 3][:, :, :].rearrange("p c (h d) -> p (c h) d", h=H),
                       bc(dv[:, :, :].rearrange("p c h -> p (c h)"), 2, 16), ALU.mult))

        def reduce_levels(ci, a, b1):
            n = ci % 4
            DV.wait(a, b1, T.get(("xbuilt", ci - 4)))
            a = DV.run(lambda e: e.tensor_reduce(Lf[n][:, :, :], lfp[:, :].rearrange("p (h s l) -> p h s l", h=H, s=16),
                                                 AX.X, ALU.add))
            b1 = DV.run(lambda e: e.tensor_reduce(Lc[n][:, :, :], lcp[:, :].rearrange("p (h s l) -> p h s l", h=H, s=8),
                                                  AX.X, ALU.add))
            T["red"] = b1
            DV.wait(a, b1)
            DV.run(tt(Lf[n][:, :, :], Lf[n][:, :, :], bc(cs[:, C_NF:C_NF + 16], 1, H), ALU.add))
            T["L", ci] = DV.run(tt(Lc[n][:, :, :], Lc[n][:, :, :], bc(cs[:, C_NC:C_NC + 8], 1, H), ALU.add))

        def exponents(G):
            ci, g = G // 4, G % 4
            c, h0, i = ci % 2, heads_of(G % 4)[0], G % 3
            x4 = X[i][:, :].rearrange("p (h b s) -> p h b s", h=4, b=8)
            GP.wait(T["L", ci], T.get(("xt", G - 3)))
            a = GP.run(tt(x4, bc(Lf[ci % 4][:, h0:h0 + 7:2, :], 2, 8),
                          cs[:, C_OWN:C_OWN + 8].unsqueeze(1).unsqueeze(3).broadcast_to([P, 4, 8, 16]), ALU.mult))
            GP.wait(a)
            T["x", G] = GP.run(tt(x4, x4, bc(Lc[ci % 4][:, h0:h0 + 7:2, :], 3, 16), ALU.add))
            if g == 3:
                T["xbuilt", ci] = T["x", G]

        def qk_ready(sg):
            return [T["QT", sg, 6], T["KT", sg, 7]]

        def scores(G):
            ci, g, i = G // 4, G % 4, G % 2
            sg, c, b = ci // 2, ci % 2, (ci // 2) % 2
            hs = heads_of(g)
            r = 64 * (hs[0] % 2)
            PE.wait(T.get(("w", G - 2)), *qk_ready(sg))
            T["p", G] = PE.run(*[
                mm(PB[i][:, 128 * n:128 * n + 128], KT[b][r:r + 64, h // 2, 128 * c:128 * c + 128],
                   QT[b][r:r + 64, h // 2, 128 * c:128 * c + 128]) for n, h in enumerate(hs)])
            PE.wait(T["x", G], T.get(("e", G - 1)))
            T["xt", G] = PE.run(*[tr(XB[:, 128 * n:128 * n + 128], X[G % 3][:, 128 * n:128 * n + 128])
                                  for n in range(4)])
            AC.wait(T["xt", G], T["ncg", sg], T.get(("w", G - 2)))
            T["e", G] = AC.run(*[act(E[i][:, 128 * n:128 * n + 128], XB[:, 128 * n:128 * n + 128], ACT.Exp,
                                     bias=ncg[b][:, c, h:h + 1]) for n, h in enumerate(hs)])
            if c == 1 and g == 3:
                T["exp", sg] = T["e", G]

        def weights(G):
            i = G % 2
            DV.wait(T["p", G], T["e", G], T.get(("y", G - 2)))
            T["w", G] = DV.run(tt(W[i][:, :], PB[i][:, :], E[i][:, :], ALU.mult))

        def weigh(G):
            ci, g, i = G // 4, G % 4, G % 2
            sg, c, b = ci // 2, ci % 2, (ci // 2) % 2
            waits = [T["w", G], T["V", sg]]
            if g == 0:
                waits.append(free[f"Y{ci % 2}"])
            T["y", G], = yield [(waits, [mm(YB[ci % 2][:, 16 * h:16 * h + 16], W[i][:, 128 * n:128 * n + 128],
                                            V[sg % 3][:, c, 16 * h:16 * h + 16]) for n, h in enumerate(heads_of(g))])]
            if c == 1 and g == 3:
                T["wv", sg] = T["y", G]

        def keys(ci):
            sg, c, b = ci // 2, ci % 2, (ci // 2) % 2
            ms = [misc() for n in range(2)]
            dones = yield [(qk_ready(sg) + [w], [tr(B[:, 128 * q:128 * q + 128], KT[b][:, 4 * n + q, 128 * c:128 * c + 128])
                                                for q in range(4)]) for n, (m, B, w) in enumerate(ms)]
            for n, ((m, B, w), done) in enumerate(zip(ms, dones)):
                AC.wait(done, T.get("kt_used"))
                free[m] = AC.run(act(Kt[:, 512 * n:512 * n + 512], B[:, :], ACT.Copy))
            T["kt"] = free[m]

        def inter(ci):
            cc = ci % CB
            sg, c, b = ci // 2, ci % 2, (ci // 2) % 2
            nb = cc.bit_length()
            if nb == 0:
                return
            zs, ms, jobs = [], [], []
            for e2 in range(2):
                m, B, wb = misc()
                ms.append(m)
                jobs.append(([T["Sd"], wb], [
                    mm(B[:, 128 * p:128 * p + 32 * nb], QT[b][:, 4 * e2 + p, 128 * c:128 * c + 128],
                       Sd[:, 4 * e2 + p, :, 0:16 * nb]) for p in range(4)]))
            dones = yield jobs
            for e2, (m, done) in enumerate(zip(ms, dones)):
                B = MB[m]
                DV.wait(done, T["coef", sg], T.get("zr_done"))
                n = 8 * nb * 16
                for e in range(2):
                    zv = zt[:, n * e2:n * e2 + n].rearrange("p (q e n) -> p q e n", q=4, e=2)[:, :, e, :]
                    zsrc = B[:, :].rearrange("p (q n) -> p q n", q=4)[:, :, 16 * nb * e:16 * nb * e + 16 * nb]
                    free[m] = DV.run(tt(zv.rearrange("p q (b d) -> p q b d", d=16),
                                        zsrc.rearrange("p q (b d) -> p q b d", d=16),
                                        bc(coef[b][:, c, 8 * e2 + e:8 * e2 + 8:2, 0:nb], 3, 16), ALU.mult))
                zs.append(free[m])
            T["S_read"] = done
            if c == 1:
                T["inter", sg] = free[m]
            DV.wait(*zs, T.get(("yf", ci - 2)))
            T["zr", ci] = T["zr_done"] = DV.run(lambda e: e.tensor_reduce(
                zr[ci % 2][:, :].rearrange("p (h d) -> p h d", d=16),
                zt[:, 0:16 * nb * 16].rearrange("p (h b d) -> p h d b", h=H, d=16), AX.X, ALU.add))

        def state(ci):
            cc = ci % CB
            sg, c, b = ci // 2, ci % 2, (ci // 2) % 2
            if cc < CB - 1:
                nb, z = cc.bit_length(), ((cc + 1) & -(cc + 1)).bit_length() - 1
                m, B, wb = misc()
                done, = yield [([T["kt"], T["Vw", sg], wb],
                                [mm(B[:, 32 * p:32 * p + 32], Kt[:, 128 * p:128 * p + 128],
                                    Vw[b][:, c, 32 * p:32 * p + 32]) for p in range(8)])]
                T["kt_used"] = done
                DV.wait(T["dec", sg], T.get("Sd"), T.get("S"))
                a = None
                if nb:
                    s3 = S[:, :, 0:nb, :].rearrange("p q b d -> p q (b d)")
                    a = DV.run(tt(s3, s3, bc(dec[b][:, c, :], 2, 16 * nb), ALU.mult))
                DV.wait(done, a)
                for e2 in range(2):
                    r = slice(64 * e2, 64 * e2 + 64)
                    src = B[r, 0:256].rearrange("p (q n) -> p q n", q=8)[:, :, 16 * e2:16 * e2 + 16]
                    if z == 0:
                        a = DV.run(cp(S[r, :, 0, :], src))
                    else:
                        a = DV.run(tt(S[r, :, z, :], src, S[r, :, 0, :], ALU.add))
                free[m] = a
                for l in range(1, z):
                    DV.wait(a)
                    a = DV.run(tt(S[:, :, z, :], S[:, :, z, :], S[:, :, l, :], ALU.add))
                if z:
                    DV.wait(a)
                    a = DV.run(lambda e: e.memset(S[:, :, 0:z, :], 0.0))
                T["S"] = a
                AC.wait(a, T.get("S_read"), T["Sd0"])
                nx = (cc + 1).bit_length()
                for e2 in range(2):
                    r = slice(64 * e2, 64 * e2 + 64)
                    T["Sd"] = AC.run(act(Sd[r, :, e2, 0:16 * nx], S[r, :, 0:nx, :].rearrange("p q b d -> p q (b d)"),
                                         ACT.Copy))
                if c == 1:
                    T["state", sg] = a
            elif c == 1:
                T["state", sg] = T["S"]

        def gather(ci):
            cc = ci % CB
            DV.wait(T["y", 4 * ci + 3], T.get("yt_done"))
            if cc:
                DV.wait(T["zr", ci])
                T["yf", ci] = DV.run(tt(yf[:, :], YB[ci % 2][:, 0:256], zr[ci % 2][:, :], ALU.add))
            else:
                T["yf", ci] = DV.run(cp(yf[:, :], YB[ci % 2][:, 0:256]))
            free[f"Y{ci % 2}"] = T["yf", ci]

        def turn_y(ci):
            done, = yield [([free[f"Y{ci % 2}"], T["yf", ci]], [
                tr(YB[ci % 2][:, 128 * k:128 * k + 128], yf[:, 128 * k:128 * k + 128]) for k in range(2)])]
            T["yt_done"] = done
            AC.wait(done, T.get("op_done"))
            free[f"Y{ci % 2}"] = T["yt"] = AC.run(act(yt[:, :], YB[ci % 2][:, 0:256], ACT.Copy))

        def norm(o, i, st, mv, lr, rs, key, used):
            a = DV.run(lambda e: e.bn_stats(st[:, :], i))
            DV.wait(a, used)
            a = DV.run(lambda e: e.bn_aggr(mv[:, :], st[:, :]))
            GP.wait(a, l_cst)
            a = GP.run(tt(lr[:, :], mv[:, 1:2], cs[:, C_EPS:C_EPS + 1], ALU.add))
            GP.wait(a)
            T[key] = GP.run(tt(rs[:, :], lr[:, :], cs[:, C_HALF:C_HALF + 1], ALU.pow))

        def out_proj(ci):
            done, = yield [([free[f"Y{ci % 2}"], T["yt"], l_wo], [
                mm(YB[ci % 2][:, 0:256], yt[:, 128 * k:128 * k + 128], wo[:, k, :], start=(k == 0), stop=(k == 1)) for k in range(2)])]
            T["op_done"] = done
            DV.wait(done, l_x[ci // 2])
            free[f"Y{ci % 2}"] = DV.run(tt(oo[:, :], YB[ci % 2][:, 0:256], xs[:, ci, :], ALU.add))
            DV.wait(free[f"Y{ci % 2}"])
            norm(None, oo[:, :], st1, mv1, lr1, rs1, "rs1", None)

        def normalise(ci):
            DV.wait(T["rs1"], T.get("nn_used"))
            a = DV.run(stt(nn[:, :], oo[:, :], mv1[:, 0:1], bv[:, B_G:B_G + 256], ALU.subtract, ALU.mult))
            DV.wait(a)
            a = DV.run(stt(nn[:, :], nn[:, :], rs1[:, 0:1], bv[:, B_B:B_B + 256], ALU.mult, ALU.add))
            GP.wait(a, l_x[ci // 2], T.get("x1_used"))
            T["x1"] = T["nn_used"] = GP.run(tt(x1[:, :], nn[:, :], xs[:, ci, :], ALU.add))

        def outer_stats(ci):
            DV.wait(T["x1"])
            norm(None, x1[:, :], st2, mv2, lr2, rs2, "rs2", None)

        def outer_norm(ci):
            DV.wait(T["rs2"])
            T["x2", ci] = T["x1_used"] = DV.run(
                ts(xs[:, ci, :], x1[:, :], mv2[:, 0:1], rs2[:, 0:1], ALU.subtract, ALU.mult))

        def together(parts):
            jobs = [next(p, None) for p in parts]
            tokens = PE.weave(*[q for js in jobs for q in js or []])
            for p, js in zip(parts, jobs):
                if js is not None:
                    mine, tokens = tokens[:len(js)], tokens[len(js):]
                    try:
                        p.send(mine)
                    except StopIteration:
                        pass

        tail = {5: gather, 9: normalise, 10: outer_stats, 12: outer_norm}
        turned = {7: turn_y, 8: out_proj}
        WF, WI, WC, UF, UI, UC, WO, UO = range(8)
        ring = [banks[0:3], [banks[3], banks[6], banks[7]]]
        bank_free = [[None] * 3, [None] * 3]
        c0 = fvs[:, 6:8]
        ov = out.rearrange("(t n p) d -> p t n d", t=2, p=P)
        s_out = sem("s_out")

        def wcol(n, mt=None):
            return slice(256 * n + 128 * mt, 256 * n + 128 * mt + 128) if mt is not None else slice(256 * n, 256 * n + 256)

        def load_ffn(n):
            SY.wait(T["split", NSG - 1], T.get(("wf", n - 3)))
            T["l_wf", n] = load(f"l_wf{n}", (xt[n % 3][:, :, :], wffn.rearrange("(k p) w n -> p k w n", p=P)[:, :, n, :]))

        def split_ffn(n):
            T["wf", n] = split(wH[:, :, wcol(n)], wL[:, :, wcol(n)], xt[n % 3][:, :, :],
                               [T["l_wf", n], T["projected", NSG - 1]])

        def first_bias():
            bank_free[0] = [free["Q0"], T["w", 4 * NC - 2], T["w", 4 * NC - 1]]
            bank_free[1] = [T["e", 4 * NC - 1], free[0], free[1]]
            over = [T["y", 4 * NC - 1], T["yf", NC - 1], T["e", 4 * NC - 1], T["x", 4 * NC - 1]]
            for e in (PE, DV, AC, GP):
                e.wait(*over)
            PE.wait(*bank_free[0], T["wf", 7], T["c0"])
            for B, c in ((banks[0][:, :], slice(256 * UF, 256 * UF + 512)), (banks[1][:, 0:256], wcol(UC))):
                done = PE.run(*[f for k in range(2) for f in mm3(B, c0H[:, k, :], c0L[:, k, :], wH[:, k, c],
                                                                 wL[:, k, c], k == 0, k == 1)])
            DV.wait(done, l_cst)
            d0, d1 = hh[0][:, :].rearrange("p (n t) -> p n t", t=128), cu[0][:, :].rearrange("p (n t) -> p n t", t=128)
            bank_free[0][0] = DV.run(tt(d0, banks[0][:, :].rearrange("p (n t) -> p n t", t=128), bc(ident, 1, 4),
                                        ALU.mult))
            a = bank_free[0][1] = DV.run(tt(d1, banks[1][:, 0:256].rearrange("p (n t) -> p n t", t=128),
                                            bc(ident, 1, 2), ALU.mult))
            bv0 = b0[:, :, :].rearrange("p m n -> p n m")
            DV.wait(a)
            DV.run(lambda e: e.tensor_reduce(bv0[:, 0:2, :], d0.rearrange("p (n m) t -> p n m t", m=2), AX.X, ALU.add))
            a = DV.run(lambda e: e.tensor_reduce(bv0[:, 2:3, :], d1.rearrange("p (n m) t -> p n m t", m=2), AX.X,
                                                 ALU.add))
            DV.wait(a)
            b0f = b0[:, :, :].rearrange("p m n -> p (m n)")
            T["b0"] = DV.run(tt(b0f, b0f, fvs[:, 0:6], ALU.add))

        def turn_block(blk, t):
            i = blk % 2
            for k in range(2):
                PE.wait(free[f"Y{k}"], *[T["x2", 16 * t + 4 * blk + q] for q in range(4)])
                done = PE.run(*[tr(banks[4 + k][:, 128 * q:128 * q + 128],
                                   xs[:, 16 * t + 4 * blk + q, 128 * k:128 * k + 128]) for q in range(4)])
                T["y", t, blk] = free[f"Y{k}"] = split(yH[t][i][:, k, :], yL[t][i][:, k, :], banks[4 + k][:, :],
                                                       [done, T.get(("out", blk - 2))], DV)

        def gates(blk, t, mt):
            i, y = mt, blk % 2
            res = []
            for n in range(3):
                PE.wait(bank_free[i][n], T["y", t, blk])
                ops = [(wH[:, k, wcol(WF + n, mt)], wL[:, k, wcol(WF + n, mt)], yH[t][y][:, k, :], yL[t][y][:, k, :])
                       for k in range(2)]
                if t:
                    ops += [(wH[:, k, wcol(UF + n, mt)], wL[:, k, wcol(UF + n, mt)], c1H[y][:, k, :], c1L[y][:, k, :])
                            for k in range(2)]
                ins = [f for q, o in enumerate(ops) for f in mm3(ring[i][n][:, :], *o, q == 0, q == len(ops) - 1)]
                if t:
                    PE.todo += ins[:6]
                    PE.wait(T["c1", blk, 0], T["c1", blk, 1])
                    ins = ins[6:]
                done = PE.run(*ins)
                AC.wait(done, T["b0"], T.get(("cell", i)))
                bias = fvs[:, 3 * mt + n:3 * mt + n + 1] if t else b0[:, mt, n:n + 1]
                bank_free[i][n] = AC.run(act(gb[i][n][:, :], ring[i][n][:, :], ACT.Tanh if n == 2 else ACT.Sigmoid,
                                             bias=bias))
                res.append(bank_free[i][n])
            DV.wait(*res)
            a = DV.run(tt(gb[i][1][:, :], gb[i][1][:, :], gb[i][2][:, :], ALU.mult))
            if t == 0:
                DV.wait(a, T.get(("gates1", blk - 2)), T.get(("c1", blk - 2, mt)))
                a = T["cell", i] = DV.run(stt(c1[y][:, mt, :], gb[i][0][:, :], c0[:, mt:mt + 1], gb[i][1][:, :],
                                              ALU.mult, ALU.add))
                T["c1", blk, mt] = split(c1H[y][:, mt, :], c1L[y][:, mt, :], c1[y][:, mt, :],
                                         [a, T.get(("gates1", blk - 2))])
            else:
                a1 = DV.run(tt(gb[i][0][:, :], gb[i][0][:, :], c1[y][:, mt, :], ALU.mult))
                DV.wait(a, a1)
                a = DV.run(tt(gb[i][1][:, :], gb[i][0][:, :], gb[i][1][:, :], ALU.add))
                T["cell", i] = T["c2", blk, mt] = split(c2H[y][:, mt, :], c2L[y][:, mt, :], gb[i][1][:, :],
                                                        [a, T.get(("out", blk - 2))], DV if blk == 3 else GP)
                T["gates1", blk] = done

        def outputs(blk, q, slots):
            tt_ = 4 * blk + q
            i = tt_ % 2
            y = blk % 2
            c = slice(128 * q, 128 * q + 128)
            (Ba, fa), (Bb, fb) = [(s[0], s[1]) for s in slots]
            PE.wait(fa(), T["c2", blk, 0], T["c2", blk, 1])
            done = PE.run(*[f for k in range(2) for f in mm3(Ba[:, 0:256], c2H[y][:, k, c], c2L[y][:, k, c],
                                                             wH[:, k, wcol(UO)], wL[:, k, wcol(UO)], k == 0, k == 1)])
            DV.wait(done, T.get(("cu", i)))
            a0 = DV.run(tt(cu[i][:, :], Ba[:, 0:256], bv[:, B_BO:B_BO + 256], ALU.add))
            slots[0][2](a0)
            PE.wait(fb())
            done = PE.run(*[f for t in range(2) for k in range(2) for f in mm3(
                Bb[:, 256 * t:256 * t + 256], yH[t][y][:, k, c], yL[t][y][:, k, c],
                wH[:, k, wcol(WO)], wL[:, k, wcol(WO)], k == 0, k == 1)])
            h3 = hh[i][:, :].rearrange("p (t n) -> p t n", t=2)
            DV.wait(done, a0, T.get(("hh", i)))
            T["cu", i] = DV.run(tt(h3, Bb[:, :].rearrange("p (t n) -> p t n", t=2), bc(cu[i][:, :], 1, 2), ALU.add))
            slots[1][2](T["cu", i])
            AC.wait(T["cu", i])
            a = AC.run(act(hh[i][:, :], hh[i][:, :], ACT.Tanh))
            GP.wait(a)
            dst = xs[:, tt_:tt_ + 17:16, :]
            T["hh", i] = GP.run(tt(dst, dst, h3, ALU.add))
            T["out", blk] = done

        def out_stats(tt_):
            i = tt_ % 2
            DV.wait(T["hh", i])
            s2 = [DV.run(lambda e, t=t: e.bn_stats(st3[:, 2 * i + t, :], xs[:, tt_ + 16 * t, :])) for t in range(2)]
            DV.wait(*s2)
            for t in range(2):
                a = DV.run(lambda e, t=t: e.bn_aggr(mv3[:, tt_ + 16 * t, :], st3[:, 2 * i + t, :]))
            GP.wait(a)
            two = slice(tt_, tt_ + 17, 16)
            a = GP.run(tt(lr3[:, two], mv3[:, two, 1], cs[:, C_EPS:C_EPS + 1].broadcast_to([P, 2]), ALU.add))
            GP.wait(a)
            T["rs3", tt_] = GP.run(tt(rs3[:, two], lr3[:, two], cs[:, C_HALF:C_HALF + 1].broadcast_to([P, 2]), ALU.pow))

        def out_norm(tt_):
            DV.wait(T["rs3", tt_])
            for t in range(2):
                n = tt_ + 16 * t
                a = DV.run(ts(xs[:, n, :], xs[:, n, :], mv3[:, n, 0:1], rs3[:, n:n + 1], ALU.subtract, ALU.mult))
            SY.wait(a)
            SY.todo.append(lambda e: e.dma_start(ov[:, :, tt_, :], xs[:, tt_:tt_ + 17:16, :]).then_inc(s_out, 16))

        def output_stage(n):
            if 0 <= n < 16:
                if n < 12:
                    slots = [(banks[4 + y], lambda y=y: free[f"Y{y}"], lambda v, y=y: free.__setitem__(f"Y{y}", v))
                             for y in range(2)]
                else:
                    i = n % 2
                    slots = [(ring[i][y], lambda y=y, i=i: bank_free[i][y],
                              lambda v, y=y, i=i: bank_free[i].__setitem__(y, v)) for y in range(2)]
                outputs(n // 4, n % 4, slots)
            if 0 <= n - 1 < 16:
                out_stats(n - 1)
            if 0 <= n - 2 < 16:
                out_norm(n - 2)

        units = [("t", 0, 0), ("t", 0, 1), ("g", 0, 0, 0), ("g", 0, 0, 1)]
        for blk in range(4):
            def o(k):
                return ("o", 4 * blk - 4 + k) if 4 * blk - 4 + k >= 0 and blk + k // 4 > 0 else None
            if blk < 3:
                units += [u for u in (("g", blk, 1, 0), o(3), ("t", blk + 1, 0), ("g", blk, 1, 1),
                                      ("t", blk + 1, 1), ("g", blk + 1, 0, 0), o(4), ("g", blk + 1, 0, 1), o(5), o(6)) if u]
            else:
                units += [("g", blk, 1, 0), ("g", blk, 1, 1), o(3)]
        n = 12
        while n < 18:
            units.append(("o", n))
            n += 1

        def unit():
            u = units.pop(0)
            if u[0] == "g":
                gates(*u[1:])
            elif u[0] == "t":
                turn_block(*u[1:])
            else:
                output_stage(u[1])

        NG = 4 * NC
        token_steps = [(11, 7), (0, 0), (0, 1), (1, 2), (3, 8), (4, 3), (5, 4), (6, 5)]
        split_wt()
        split_x(0)
        AC.wait(l_cst)
        T["eA"] = AC.run(act(eA[:, :], bv[:, B_AL:B_AL + H], ACT.Exp))
        for s in range(-17, NG + 13):
            sg, j = (s + 9) // 8, (s + 9) % 8
            if 0 <= s - 1 < NG:
                weights(s - 1)
            products = T.pop("todo", None)
            if 0 <= s < NG:
                scores(s)
                if s % 8 == 7:
                    T["heads", s // 8] = T["p", s]
            parts = []
            if 1 <= sg < NSG:
                parts.append(project(sg, j))
            if s in (-12, -11, -10, -8):
                n = (-12, -11, -10, -8).index(s)
                parts += [project(0, 2 * n + k) for k in range(2)]
            if s % 8 == 7 and 1 <= (s + 17) // 8 < NSG:
                split_x((s + 17) // 8)
            if s in (-15, -14):
                split_wq(2 * (s + 15), DV)
            if s == -11:
                split_wq(1, GP)
                split_wq(3, GP)
            if 0 <= s - NG + 10 < 8:
                load_ffn(s - NG + 10)
            if 0 <= s - NG + 8 < 8:
                split_ffn(s - NG + 8)
            if s == NG - 4:
                T["c0"] = split(c0H[:, :, :], c0L[:, :, :], bc(c0, 2, 128), [l_cst])
            if s == NG + 2:
                first_bias()
                unit()
                unit()
            if s >= NG + 3:
                unit()
            if 0 <= s < NG and s % 4 < 3:
                parts.append([keys, inter, state][s % 4](s // 4))
            if 0 <= s - 2 < NG:
                parts.append(weigh(s - 2))
            if 0 <= s + 2 < NG:
                exponents(s + 2)
            for d, f in turned.items():
                if s - d >= 0 and (s - d) % 4 == 0 and (s - d) // 4 < NC:
                    parts.append(f((s - d) // 4))
            for d, j in token_steps:
                n = s + 13 - d
                if n + 2 == 8 and d <= 4:
                    parts.append(tokens(1, j))
                elif n % 8 == 0 and 0 <= n // 8 < NSG and not (n == 8 and d <= 4):
                    parts.append(tokens(n // 8, j))
            together(parts)
            for d, f in tail.items():
                if s - d >= 0 and (s - d) % 4 == 0 and (s - d) // 4 < NC:
                    f((s - d) // 4)
            if products:
                reduce_levels(*products)

        while units:
            unit()
        SY.wait((s_out, 16 * 16))

        block = ctx.enter_context(nc.Block())

        @block.sync
        def _(e):
            SY.replay(e)

        @block.tensor
        def _(e):
            PE.replay(e)

        @block.vector
        def _(e):
            DV.replay(e)

        @block.scalar
        def _(e):
            AC.replay(e)

        @block.gpsimd
        def _(e):
            GP.replay(e)


def constants():
    c = np.zeros((P, C_END), np.float32)
    t = np.arange(P)
    c[:, C_TRI:C_TRI + 128] = t[:, None] <= t[None, :]
    c[:, C_ONE:C_ONE + 128] = 1.0
    c[:, C_ID:C_ID + 128] = np.eye(P)

    def level(a, b):
        v = a ^ b
        return int(v).bit_length()

    for p in range(P):
        for b in range(8):
            k = p // 16
            if b < k:
                c[p, C_MC + 3 * b + level(k, b) - 1] = 1.0
            if b > k:
                c[p, C_NC + b] = NEG
            if b == k:
                c[p, C_OWN + b] = 1.0
        for s in range(16):
            if s <= p % 16:
                c[p, C_MF + 5 * s + level(p % 16, s)] = 1.0
            else:
                c[p, C_NF + s] = NEG
    c[:, C_EPS] = EPS
    c[:, C_HALF] = -0.5
    return c


def kernel(**a):
    import concourse.bacc as bacc
    from concourse.bass_utils import run_bass_kernel_spmd

    a = {k: np.asarray(v) for k, v in a.items()}
    f = {k.replace("L0_attn_", "").replace("L0_ffn_", "f_"): v for k, v in a.items()}
    x = np.ascontiguousarray(f["x"].reshape(NT, 256))
    dlt = np.concatenate([f["Wdl"].reshape(H, LV, 256), f["Wdt"].reshape(H, 1, 256)], 1).reshape(H * NL, 256)
    lp = np.concatenate([f["Lp"], np.ones((H, 1), np.float32)], 1).reshape(-1)
    bi = np.concatenate([np.zeros((H, LV), np.float32), f["dt_bias"].reshape(H, 1)], 1).reshape(-1)
    row = np.concatenate([lp, bi, f["A_log"], f["ln_g"], f["ln_b"], f["f_bo"]])
    fv = np.concatenate([np.stack([f["f_bf"], f["f_bi"], f["f_bc"]], 1).reshape(2, P, 3).transpose(1, 0, 2).reshape(P, 6),
                         f["f_in_c"].reshape(2, P).T], 1)
    data = {
        "x": x,
        "xT": x.T,
        "wqk": np.concatenate([f["Wq"], f["Wk"]], 0).T,
        "wtok": np.concatenate([f["Wv"], dlt], 0).T,
        "wout": f["Wout"].T,
        "wffn": np.stack([f["f_" + n].T for n in ("wf", "wi", "wc", "uf", "ui", "uc", "wo", "uo")], 1),
        "cst": constants(),
        "bcv": np.broadcast_to(row, (P, B_END)),
        "fv": fv,
    }
    data = {k: np.ascontiguousarray(v) for k, v in data.items()}
    nc = bacc.Bacc("TRN2", target_bir_lowering=False, num_devices=1)
    aps = [nc.dram_tensor("in_" + k, v.shape, F32, kind="ExternalInput").ap() for k, v in data.items()]
    aps.append(nc.dram_tensor("out_0", (NT, 256), F32, kind="ExternalOutput").ap())
    program(nc, *aps)
    r = run_bass_kernel_spmd(nc, [{"in_" + k: v for k, v in data.items()}], core_ids=[0])
    return r.results[0]["out_0"].reshape(2, 2048, 256)
```
